# Optimizing a Trainium2 kernel written in Bass

```python
import numpy as np
import jax
import jax.numpy as jnp

def _softmax(x, axis=-1):
    return jax.nn.softmax(x, axis=axis)

def _gelu(x):
    return jax.nn.gelu(x, approximate=True)

def _silu(x):
    return jax.nn.silu(x)

def _sigmoid(x):
    return jax.nn.sigmoid(x)

def _layernorm(x, axis=-1, eps=1e-05):
    m = jnp.mean(x, axis=axis, keepdims=True)
    v = jnp.var(x, axis=axis, keepdims=True)
    return (x - m) / jnp.sqrt(v + eps)

def _scatter_add(tgt, idx, src, axis=0):
    return tgt.at[idx].add(src)

def _segment_sum(src, seg, n):
    return jax.ops.segment_sum(src, seg, n)
kernel_name = 'mk_vit_tower_cls_d1_tok_img768_r4_4bf7af'

def setup_inputs(seed: int=0):
    np.random.seed(seed)
    _w = jnp.asarray

    def _rec_inputs():
        import jax
        import jax.numpy as jnp
        _rk = jax.random.key(seed)
        x = -0.000596345 + 1.00056 * jax.random.normal(jax.random.fold_in(_rk, 1), (4, 3, 64, 64), jnp.float32)
        cls_tok = 0.02 * jax.random.normal(jax.random.fold_in(_rk, 5), (1, 1, 192), jnp.float32)
        return (x, cls_tok)
    x, cls_tok = _rec_inputs()

    def _L0_tok_setup():
        import jax, jax.numpy as jnp
        import numpy as np
        B = 16
        IMG = 64
        CH = 3
        EMBED = 64
        GP = 16
        PRE = [1, 2, 4]
        N_LEVELS = 3
        FUSED = EMBED * N_LEVELS

        def hilbert_flat_indices(n):
            t = np.arange(n * n, dtype=np.int64)
            x = np.zeros(n * n, dtype=np.int64)
            y = np.zeros(n * n, dtype=np.int64)
            s = 1
            while s < n:
                rx = 1 & t // 2
                ry = 1 & (t ^ rx)
                swap = ry == 0
                flip = swap & (rx == 1)
                x = np.where(flip, s - 1 - x, x)
                y = np.where(flip, s - 1 - y, y)
                x2 = np.where(swap, y, x)
                y2 = np.where(swap, x, y)
                x, y = (x2, y2)
                x = x + s * rx
                y = y + s * ry
                t = t // 4
                s *= 2
            return y * n + x

        def _level(x, idx, W, b, p, gp):
            Bsz, C, H, _ = x.shape
            h = H // p
            t = x.reshape(Bsz, C, h, p, h, p).transpose(0, 2, 4, 3, 5, 1).reshape(Bsz, h * h, p * p * C)
            t = t[:, idx]
            t = t.reshape(Bsz, h * h // gp, gp * p * p * C)
            return t @ W.T + b

        def _interp_linear(x, n_out):
            L = x.shape[1]
            pos = (jnp.arange(n_out, dtype=jnp.float32) + 0.5) * (L / n_out) - 0.5
            pos = jnp.clip(pos, 0.0, L - 1)
            i0 = jnp.floor(pos).astype(jnp.int32)
            i1 = jnp.minimum(i0 + 1, L - 1)
            w = (pos - i0).astype(x.dtype)
            return x[:, i0] * (1.0 - w)[None, :, None] + x[:, i1] * w[None, :, None]
        key = jax.random.key(seed)
        ks = jax.random.split(key, 9)
        inp = {'x': jax.random.normal(ks[0], (B, CH, IMG, IMG), jnp.float32)}
        for i, p in enumerate(PRE):
            din = CH * p * p * GP
            inp[f'W{i}'] = jax.random.normal(ks[1 + 2 * i], (EMBED, din), jnp.float32) * din ** (-0.5)
            inp[f'b{i}'] = jax.random.normal(ks[2 + 2 * i], (EMBED,), jnp.float32) * 0.02
        inp['Wf'] = jax.random.normal(ks[7], (FUSED, FUSED), jnp.float32) * FUSED ** (-0.5)
        inp['bf'] = jax.random.normal(ks[8], (FUSED,), jnp.float32) * 0.02
        for i, p in enumerate(PRE):
            inp[f'idx{i}'] = jnp.asarray(hilbert_flat_indices(IMG // p), jnp.int32)
        return inp
    _L0_tok_all = _L0_tok_setup()
    _L0_tok_in = {k: v for k, v in _L0_tok_all.items() if k in ('W0', 'b0', 'W1', 'b1', 'W2', 'b2', 'Wf', 'bf', 'idx0', 'idx1', 'idx2')}
    del _L0_tok_all

    def _L0_attn_setup():
        import jax, jax.numpy as jnp
        import numpy as np
        NUM_HEADS = 8
        key = jax.random.key(seed)
        k1, k2, k3, k4 = jax.random.split(key, 4)
        B, N, C = (2, 1024, 192)
        x = jax.random.normal(k1, (B, N, C), dtype=jnp.float32)
        w_qkv = jax.random.normal(k2, (C, 3 * C), dtype=jnp.float32) * C ** (-0.5)
        w_proj = jax.random.normal(k3, (C, C), dtype=jnp.float32) * C ** (-0.5)
        b_proj = jax.random.normal(k4, (C,), dtype=jnp.float32) * 0.02
        return {'x': x, 'w_qkv': w_qkv, 'w_proj': w_proj, 'b_proj': b_proj}
    _L0_attn_all = _L0_attn_setup()
    _L0_attn_in = {k: v for k, v in _L0_attn_all.items() if k in ('w_qkv', 'w_proj', 'b_proj')}
    del _L0_attn_all

    def _L0_ffn_setup():
        import jax, jax.numpy as jnp
        import numpy as np
        S, B, DIM = (256, 4, 192)
        N_EXPERTS = 8
        HID = 512
        key = jax.random.key(seed)
        ks = jax.random.split(key, 6)
        scale = 0.02
        return {'hidden_states': jax.random.normal(ks[0], (S, B, DIM), dtype=jnp.float32), 'router_w': jax.random.normal(ks[1], (DIM, N_EXPERTS), dtype=jnp.float32) * scale, 'router_b': jnp.zeros((N_EXPERTS,), dtype=jnp.float32), 'w1': jax.random.normal(ks[2], (N_EXPERTS, DIM, HID), dtype=jnp.float32) * scale, 'w2': jax.random.normal(ks[3], (N_EXPERTS, DIM, HID), dtype=jnp.float32) * scale, 'w3': jax.random.normal(ks[4], (N_EXPERTS, HID, DIM), dtype=jnp.float32) * scale}
    _L0_ffn_all = _L0_ffn_setup()
    _L0_ffn_in = {k: v for k, v in _L0_ffn_all.items() if k in ('router_w', 'router_b', 'w1', 'w2', 'w3')}
    del _L0_ffn_all
    return {'x': x, 'cls_tok': cls_tok, 'L0_tok_W0': _L0_tok_in['W0'], 'L0_tok_b0': _L0_tok_in['b0'], 'L0_tok_W1': _L0_tok_in['W1'], 'L0_tok_b1': _L0_tok_in['b1'], 'L0_tok_W2': _L0_tok_in['W2'], 'L0_tok_b2': _L0_tok_in['b2'], 'L0_tok_Wf': _L0_tok_in['Wf'], 'L0_tok_bf': _L0_tok_in['bf'], 'L0_tok_idx0': _L0_tok_in['idx0'], 'L0_tok_idx1': _L0_tok_in['idx1'], 'L0_tok_idx2': _L0_tok_in['idx2'], 'L0_attn_w_qkv': _L0_attn_in['w_qkv'], 'L0_attn_w_proj': _L0_attn_in['w_proj'], 'L0_attn_b_proj': _L0_attn_in['b_proj'], 'L0_ffn_router_w': _L0_ffn_in['router_w'], 'L0_ffn_router_b': _L0_ffn_in['router_b'], 'L0_ffn_w1': _L0_ffn_in['w1'], 'L0_ffn_w2': _L0_ffn_in['w2'], 'L0_ffn_w3': _L0_ffn_in['w3']}

def reference(x, cls_tok, L0_tok_W0, L0_tok_b0, L0_tok_W1, L0_tok_b1, L0_tok_W2, L0_tok_b2, L0_tok_Wf, L0_tok_bf, L0_tok_idx0, L0_tok_idx1, L0_tok_idx2, L0_attn_w_qkv, L0_attn_w_proj, L0_attn_b_proj, L0_ffn_router_w, L0_ffn_router_b, L0_ffn_w1, L0_ffn_w2, L0_ffn_w3):
    import jax
    import jax.numpy as jnp

    def _L0_tok_ref(x, W0, b0, W1, b1, W2, b2, Wf, bf, idx0, idx1, idx2):
        import jax, jax.numpy as jnp
        import numpy as np
        B = 16
        IMG = 64
        CH = 3
        EMBED = 64
        GP = 16
        PRE = [1, 2, 4]
        N_LEVELS = 3
        FUSED = EMBED * N_LEVELS

        def hilbert_flat_indices(n):
            t = np.arange(n * n, dtype=np.int64)
            x = np.zeros(n * n, dtype=np.int64)
            y = np.zeros(n * n, dtype=np.int64)
            s = 1
            while s < n:
                rx = 1 & t // 2
                ry = 1 & (t ^ rx)
                swap = ry == 0
                flip = swap & (rx == 1)
                x = np.where(flip, s - 1 - x, x)
                y = np.where(flip, s - 1 - y, y)
                x2 = np.where(swap, y, x)
                y2 = np.where(swap, x, y)
                x, y = (x2, y2)
                x = x + s * rx
                y = y + s * ry
                t = t // 4
                s *= 2
            return y * n + x

        def _level(x, idx, W, b, p, gp):
            Bsz, C, H, _ = x.shape
            h = H // p
            t = x.reshape(Bsz, C, h, p, h, p).transpose(0, 2, 4, 3, 5, 1).reshape(Bsz, h * h, p * p * C)
            t = t[:, idx]
            t = t.reshape(Bsz, h * h // gp, gp * p * p * C)
            return t @ W.T + b

        def _interp_linear(x, n_out):
            L = x.shape[1]
            pos = (jnp.arange(n_out, dtype=jnp.float32) + 0.5) * (L / n_out) - 0.5
            pos = jnp.clip(pos, 0.0, L - 1)
            i0 = jnp.floor(pos).astype(jnp.int32)
            i1 = jnp.minimum(i0 + 1, L - 1)
            w = (pos - i0).astype(x.dtype)
            return x[:, i0] * (1.0 - w)[None, :, None] + x[:, i1] * w[None, :, None]
        Ws = [(idx0, W0, b0, PRE[0]), (idx1, W1, b1, PRE[1]), (idx2, W2, b2, PRE[2])]
        outs = [_level(x, idx, W, b, p, GP) for idx, W, b, p in Ws]
        n_tokens = outs[0].shape[1]
        outs = [outs[0]] + [_interp_linear(o, n_tokens) for o in outs[1:]]
        y = jnp.concatenate(outs, axis=-1)
        return y @ Wf.T + bf

    def _L0_attn_ref(x, w_qkv, w_proj, b_proj):
        import jax, jax.numpy as jnp
        import numpy as np
        NUM_HEADS = 8
        B, N, C = x.shape
        H = NUM_HEADS
        Dh = C // H
        scale = Dh ** (-0.5)
        qkv = (x @ w_qkv).reshape(B, N, 3, H, Dh).transpose(2, 0, 3, 1, 4)
        q, k, v = (qkv[0], qkv[1], qkv[2])
        attn = jnp.einsum('bhqd,bhkd->bhqk', q, k) * scale
        attn = jax.nn.softmax(attn, axis=-1)
        out = jnp.einsum('bhqk,bhkd->bhqd', attn, v)
        out = out.transpose(0, 2, 1, 3).reshape(B, N, C)
        return out @ w_proj + b_proj

    def _L0_ffn_ref(hidden_states, router_w, router_b, w1, w2, w3):
        import jax, jax.numpy as jnp
        import numpy as np
        S, B, DIM = (256, 4, 192)
        N_EXPERTS = 8
        HID = 512
        s, b, h = hidden_states.shape
        route = jax.nn.softmax(hidden_states @ router_w + router_b, axis=2)
        max_prob = jnp.max(route, axis=2).reshape(-1, 1)
        max_ind = jnp.argmax(route, axis=2).reshape(-1)
        x = hidden_states.reshape(-1, h)
        out = jnp.zeros_like(x)
        for e in range(N_EXPERTS):
            mask = (max_ind == e)[:, None]
            xe = jnp.where(mask, x, 0.0)
            oe = jax.nn.silu(xe @ w1[e]) * (xe @ w2[e]) @ w3[e]
            out = out + jnp.where(mask, oe, 0.0)
        out = out.astype(jnp.bfloat16) * max_prob
        return out.reshape(s, b, h)
    h = _L0_tok_ref(x, L0_tok_W0, L0_tok_b0, L0_tok_W1, L0_tok_b1, L0_tok_W2, L0_tok_b2, L0_tok_Wf, L0_tok_bf, L0_tok_idx0, L0_tok_idx1, L0_tok_idx2)
    h = jnp.concatenate([jnp.broadcast_to(cls_tok, (h.shape[0], 1, h.shape[2])), h], axis=1)
    h = h + _L0_attn_ref(_layernorm(h, axis=-1), L0_attn_w_qkv, L0_attn_w_proj, L0_attn_b_proj)
    h = h + _L0_ffn_ref(_layernorm(h, axis=-1), L0_ffn_router_w, L0_ffn_router_b, L0_ffn_w1, L0_ffn_w2, L0_ffn_w3)
    return h

_drawn_inputs = setup_inputs


def setup_inputs(seed=0):
    import zlib

    import numpy as np

    out = dict(_drawn_inputs(seed))
    spreads = {'L0_ffn_router_b': (0.0, 0.8)}
    factors = {'cls_tok': 4.621,
     'L0_tok_b0': 2.958,
     'L0_tok_b1': 3.121,
     'L0_tok_b2': 3.024,
     'L0_attn_b_proj': 2.769,
     'L0_ffn_router_w': 8.0,
     'L0_ffn_w1': 8.0,
     'L0_ffn_w2': 8.0,
     'L0_ffn_w3': 8.0}
    for name, (base, spread) in spreads.items():
        noise = np.random.default_rng([zlib.crc32(name.encode()), seed]).standard_normal(out[name].shape)
        drawn = base * np.exp(spread * noise) if base else spread * noise
        out[name] = jnp.asarray(drawn.astype(out[name].dtype))
    for name, factor in factors.items():
        out[name] = (out[name] * factor).astype(out[name].dtype)
    return out
```

```python
from contextlib import ExitStack

import concourse.bass as bass
from concourse import mybir

ALU = mybir.AluOpType
ACT = mybir.ActivationFunctionType
AX_X = mybir.AxisListType.X
F32 = mybir.dt.float32
BF16 = mybir.dt.bfloat16
I32 = mybir.dt.int32
U32 = mybir.dt.uint32

B = 4
GRID = 64
CH = 3
GP = 16
N = GRID * GRID // GP
S = N + 1
C = 192
KH = C // 2
EMB = 64
H = 8
D = C // H
HG = 4
G = H // HG
HP = 32
GH = HG * D
P = 128
HALVES = N // P
TILES = B * HALVES + 1
CLS = TILES - 1
E = 8
HID = 512
HC = HID // P
ROW = C + 4
REG = (B * S + P - 1) // P * P
SLOTS = (B * S + E * (P - 1)) // P
STEPS = 4
assert (SLOTS - 3) % STEPS == 0
PAD_ROW = E * REG
NO_ROW = 1 << 20
EPS = 1e-5
SCALE = float(D) ** -0.5

G1 = 2
G2 = 8
N1, N2 = N // 4, N // 16
V0, V1, V2 = CH, CH * 4, CH * 16
L0, L1, L2 = GP * V0, GP * V1, GP * V2
GATHERS = GP // G2 + GP // G1 + HALVES * GP
COL1 = GP // G2
COL0 = COL1 + GP // G1

K_ID = 0
K_I1 = K_ID + P
K_MQ = K_I1 + 2 * HALVES * P
K_M8 = K_MQ + HG
K_SEL = K_M8 + G * H
K_E = K_SEL + G * P
K_BASE = K_E + E
K_TRI = K_BASE + E
K_ONE = K_TRI + P
K_J = K_ONE + P
NJ = REG // P
K_LE = K_J + E * NJ
K_S = K_LE + E * E
K_S128 = K_S + SLOTS * E
K_END = K_S128 + SLOTS


def build(nc, pix0, pix1, pix2, idx, lw, wft, lb, bf, cls_tok, wqkv, wproj, bproj, rw, rb, w1, w2, w3,
          consts, interp2, out):
    with ExitStack() as ctx:
        def sb(name, shape, dt=F32):
            return ctx.enter_context(nc.sbuf_tensor(name, shape, dt))

        area = sb("area", [P, 2 * H * HALVES * S])

        def carve(at, *shape):
            n = 1
            for size in shape[1:]:
                n *= size
            names = " ".join("abcd"[:len(shape) - 1])
            sizes = dict(zip("abcd", shape[1:]))
            return area[0:shape[0], at:at + n].rearrange(f"p ({names}) -> p {names}", **sizes), at + n

        def sem(name):
            return ctx.enter_context(nc.semaphore(name))

        scratch = nc.dram_tensor("routed_rows", (PAD_ROW + P, ROW), F32, kind="Internal").ap()

        psum = ctx.enter_context(nc.psum_tensor("psum", [P, 8, 512], F32))
        bank = [psum[:, i, :] for i in range(8)]

        k = sb("k", [P, K_END])
        ident = k[:, K_ID:K_ID + P]
        idx_sb = sb("idx_sb", [P, GATHERS], I32)
        lw_sb, at = carve(0, EMB, L0 + L1 + L2)
        wft_sb, at = carve(at, EMB, 3, C)
        lb_sb = sb("lb_sb", [EMB, 3])
        lb_rep = sb("lb_rep", [EMB, 3, B * N2])
        bf_sb = sb("bf_sb", [1, C])
        wqkv_sb = sb("wqkv_sb", [KH, 2, 3 * C])
        wv_pad = sb("wv_pad", [KH, 2, H, HP])
        wproj_sb = sb("wproj_sb", [P, G, C])
        bproj_sb = sb("bproj_sb", [P, C])
        rw_sb = sb("rw_sb", [KH, 2, E])
        rb_sb = sb("rb_sb", [P, E])
        w12_sb = sb("w12_sb", [KH, E * 2 * 2 * HID])
        w3_sb = sb("w3_sb", [P, E * HC * C])
        tri_bf = sb("tri_bf", [P, P], BF16)
        one_bf = sb("one_bf", [P, P], BF16)

        px0, at = carve(at, P, HALVES * GP, B * V0)
        px1, at = carve(at, P, GP // G1, B * V1)
        px2, at = carve(at, P, GP // G2, B * V2)
        px0b, at = carve(at, P, B, GP * V0)
        px1b, at = carve(at, P, B, L1 // G1)
        px2b, at = carve(at, P, B, L2 // G2)
        px1t, at = carve(at, L1 // G1, G1, B, N1)
        px2t, at = carve(at, L2 // G2, G2, B, N2)
        c1, at = carve(at, L1 // G1, G1, C)
        c2, at = carve(at, L2 // G2, G2, C)
        tok_l, at = carve(at, P, B, HALVES, P)
        tok_r = sb("tok_r", [P, C])
        f1, at = carve(at, P, 2, C)
        cls_x = sb("cls_x", [B, C])
        stat1 = sb("stat1", [P, TILES, 6])
        mv1 = sb("mv1", [P, TILES, 2])
        half_neg = sb("half_neg", [P, TILES])
        rstd1 = sb("rstd1", [P, TILES])
        xn1 = sb("xn1", [P, B, C])
        xn1c = sb("xn1c", [B, C])
        xt1 = sb("xt1", [KH, 2, B, S])

        v_sb = sb("v_sb", [P, B, HALVES, H, HP])
        vcls = sb("vcls", [P, G, B])
        q_sb = sb("q_sb", [GH, S])
        q_head = sb("q_head", [GH, 2, G, HG, N])
        q_cls = sb("q_cls", [GH, 2, G, H])
        k_sb = sb("k_sb", [GH, 2, G, S])
        nmax = sb("nmax", [P, H, HALVES])
        den = sb("den", [P, H, HALVES])
        rp = sb("rp", [P, 2, HALVES, H])
        rp_rows = sb("rp_rows", [P, 2, HALVES, HG * HP])
        probs, at = carve(0, P, H, HALVES, S)
        pt, at = carve(at, P, H, HALVES, S)
        nmax_c = sb("nmax_c", [H, 1])
        rp_c = sb("rp_c", [H, 2])
        den_c = sb("den_c", [H, 1])
        col = sb("col", [P, HALVES, H])
        probs_c = sb("probs_c", [H, S])
        rpt = sb("rpt", [P, 2, S])
        part = sb("part", [P, S])
        ot = sb("ot", [P, B, G, S])
        rpc = sb("rpc", [P, 2, G, 2])

        rows = sb("rows", [P, TILES, ROW])
        h1 = rows[:, :, 0:C]
        rows_i = rows[:, :, :].bitcast(I32)
        stat2 = sb("stat2", [P, 2, 6])
        vare = sb("vare", [P, TILES])
        xn2 = sb("xn2", [P, 2, C])
        xt2 = sb("xt2", [KH, 2, 2, P])
        logits = sb("logits", [P, 2, E])
        top = sb("top", [P, 2, E])
        topi = sb("topi", [P, 2, E], U32)
        ntop = sb("ntop", [P, 2])
        prob_e = sb("prob_e", [P, 2, E])
        prob_s = sb("prob_s", [P, 2])
        chosen = sb("chosen", [P, TILES, E], BF16)
        place = sb("place", [P, 2, E])
        place2 = sb("place2", [P, 2, E])
        pos = sb("pos", [P, TILES])
        pos_i = sb("pos_i", [P, TILES], I32)
        empty = sb("empty", [P, 1, ROW])
        slot_f = sb("slot_f", [1, 2, SLOTS])
        slot_g = sb("slot_g", [1, SLOTS])
        slot_i = sb("slot_i", [1, 2, SLOTS], I32)

        xs, at = carve(0, P, SLOTS * ROW)
        xs_i = xs[:, :].bitcast(I32)
        xn3, at = carve(at, P, C)
        xt3, at = carve(at, KH, 2, P)
        gate, at = carve(at, P, HID)
        hid, at = carve(at, P, HID)
        hid_t, at = carve(at, P, HC, P)
        o_bf = sb("o_bf", [P, C], BF16)
        y, at = carve(at, P, C)
        y_row = sb("y_row", [P, 1], U32)

        nt, at = carve(at, 1, E * NJ + 6 * E)
        upto, at = carve(at, 1, E * E + E)
        le, at = carve(at, 1, SLOTS * E)
        wle, at = carve(at, 1, SLOTS * E)
        idx_in, lw_in, wft_in, k_in, int2_in, small_in, wqkv_in, attn_w_in, rout_w_in = (
            sem(n) for n in ("idx_in", "lw_in", "wft_in", "k_in", "int2_in", "small_in", "wqkv_in", "attn_w_in",
                             "rout_w_in"))
        w_in = [sem(f"w{e}_in") for e in range(E)]
        px2_in, px1_in = sem("px2_in"), sem("px1_in")
        px0_in = [sem(f"px0_in{i}") for i in range(HALVES)]
        px2_by_image, px1_by_image, px0_by_image = sem("px2_by_image"), sem("px1_by_image"), sem("px0_by_image")
        prep = sem("prep")
        consts_bf, lb_ready = sem("consts_bf"), sem("lb_ready")
        cw_mm, cw_ev = sem("cw_mm"), sem("cw_ev")
        clsn, cls_t, cls_ev, vcls_mm, vcls_ev = (sem(n) for n in ("clsn", "cls_t", "cls_ev", "vcls_mm", "vcls_ev"))
        px2_t, px2_ev, f2_mm, f2_ev = (sem(n) for n in ("px2_t", "px2_ev", "f2_mm", "f2_ev"))
        px1_t, px1_ev, f1_mm, f1_ev = (sem(n) for n in ("px1_t", "px1_ev", "f1_mm", "f1_ev"))
        px0_t, px0_ev = sem("px0_t"), sem("px0_ev")
        tok_mm, var1_ready, rstd1_ready, xn1_ready = (
            sem(n) for n in ("tok_mm", "var1_ready", "rstd1_ready", "xn1_ready"))
        xt1_t, xt1_ev, v_mm, v_ev = (sem(n) for n in ("xt1_t", "xt1_ev", "v_mm", "v_ev"))
        q_mm, q_in, k_mm, q_ev, k_ev, qc_ev = (sem(n) for n in ("q_mm", "q_in", "k_mm", "q_ev", "k_ev", "qc_ev"))
        sc_mm, max_ready, exp_ready, p_t, pt_dve, pt_act, pv_mm = (
            sem(n) for n in ("sc_mm", "max_ready", "exp_ready", "p_t", "pt_dve", "pt_act", "pv_mm"))
        csc_mm, cmax_ready, cexp_ready, crp_ready, cp_t, cp_ev = (
            sem(n) for n in ("csc_mm", "cmax_ready", "cexp_ready", "crp_ready", "cp_t", "cp_ev"))
        rp_rows_ready, col_ready = sem("rp_rows_ready"), sem("col_ready")
        rp_ready, rp_t, rp_ev, rpc_ready, part_ready, ot_ready = (
            sem(n) for n in ("rp_ready", "rp_t", "rp_ev", "rpc_ready", "part_ready", "ot_ready"))
        proj_mm, h2_ready, var2_ready, rstd2_ready, xn2_ready, xt2_t, xt2_ev = (
            sem(n) for n in ("proj_mm", "h2_ready", "var2_ready", "rstd2_ready", "xn2_ready", "xt2_t", "xt2_ev"))
        lg_mm, lg_ready, ntop_ready, pexp_ready, prob_ready, chosen_ready, rank_mm, place_ready, pos_ready = (
            sem(n) for n in ("lg_mm", "lg_ready", "ntop_ready", "pexp_ready", "prob_ready", "chosen_ready", "rank_mm",
                             "place_ready", "pos_ready"))
        row_ids, empty_ready, empty_out, row_out, cnt_mm, slots_ready = (
            sem(n) for n in ("row_ids", "empty_ready", "empty_out", "row_out", "cnt_mm", "slots_ready"))
        xs_in, xn3_ready, xt3_t, xt3_ev, up_mm, gate_ready, hid_ready, hid_t_t, hid_t_ev, down_mm, obf_ready, y_ready = (
            sem(n) for n in ("xs_in", "xn3_ready", "xt3_t", "xt3_ev", "up_mm", "gate_ready", "hid_ready", "hid_t_t",
                             "hid_t_ev", "down_mm", "obf_ready", "y_ready"))
        y_out, dve_done, h1_ready = (sem(n) for n in ("y_out", "dve_done", "h1_ready"))

        block = ctx.enter_context(nc.Block())

        MISC = (6, 7)
        HEADS = B * H
        PLAN = []
        for b in range(B):
            prev, nxt = b > 0, b + 1 < B
            PLAN += [
                [("ct", b)] + [("rk", b - 2)] * (b > 1),
                [("f", G * b - 1)] * prev + [("q", G * (b + 1))] * nxt,
                [("k", G * (b + 1))] * nxt,
                [("pj", b - 1)] * prev,
                [("q", G * (b + 1) + 1)] * nxt,
                [("f", G * b)] + [("k", G * (b + 1) + 1)] * nxt,
                [("cs", b + 1)] * nxt + [("xr", b - 1)] * prev,
                [("lg", b - 1)] * prev,
            ]
        PLAN += [[("rk", B - 2)], [("f", G * B - 1)], [],
                 [(kind, b) for kind in ("pj", "xr", "lg", "rk") for b in (B - 1, B)] + [("cn", 0)]]
        TURN_LAG = 2
        VALUES_LAG = 6

        FIRST = [(kind, g) for g in range(G) for kind in ("q", "k")] + [("cs", 0)]
        SPARE = {task: bank[MISC[i % 2]] for i, task in enumerate(FIRST + sum(PLAN, []))}

        def after_slots(eng, signal, s, each=1):
            if not (isinstance(s, int) and s == 0):
                eng.wait_ge(signal, s * each)

        @block.sync
        def _(sp):
            sp.dma_start(idx_sb[:, :], idx).then_inc(idx_in, 16)
            sp.dma_start(lw_sb[:, :], lw).then_inc(lw_in, 16)
            sp.dma_start(wft_sb[:, :, :], wft).then_inc(wft_in, 16)
            sp.dma_start(tok_l[L0:P, :, :, :].rearrange("p b h n -> p (b h n)"), interp2).then_inc(int2_in, 16)
            sp.dma_start(wqkv_sb[:, :, :], wqkv.rearrange("(p t) n -> p t n", t=2)).then_inc(wqkv_in, 16)
            sp.dma_start(wproj_sb[:, :, :], wproj).then_inc(attn_w_in, 16)
            sp.dma_start(rw_sb[:, :, :], rw.rearrange("(p t) n -> p t n", t=2)).then_inc(rout_w_in, 16)
            sp.dma_start(rb_sb[:, :], rb.broadcast_to([P, E])).then_inc(rout_w_in, 16)
            sp.wait_ge(empty_ready, 1)
            sp.wait_ge(px0_in[1], 16 * GP)
            for e in range(E):
                sp.dma_start(scratch[e * REG:(e + 1) * REG, :].rearrange("(p t) c -> p t c", p=P),
                             empty[:, :, :].broadcast_to([P, REG // P, ROW])).then_inc(empty_out, 16)
            sp.dma_start(scratch[PAD_ROW:PAD_ROW + P, :], empty[:, 0, :]).then_inc(empty_out, 16)
            for e in range(E):
                for i, w in enumerate((w1, w2)):
                    at = (2 * e + i) * 2 * HID
                    sp.dma_start(w12_sb[:, at:at + 2 * HID],
                                 w[e].rearrange("(p t) n -> p (t n)", t=2)).then_inc(w_in[e], 16)
                sp.dma_start(w3_sb[:, e * HC * C:(e + 1) * HC * C],
                             w3[e].rearrange("(p t) n -> p (t n)", t=HC)).then_inc(w_in[e], 16)
            sp.wait_ge(slots_ready, 1)
            sp.wait_ge(row_out, 16 * TILES)
            def load_slot(s):
                first = sp.value_load(slot_i[0:1, 1, bass.ds(s, 1)], min_val=0, max_val=PAD_ROW)
                after_slots(sp, xs_in, s, 16)
                sp.dma_start(xs[:, bass.ds(s * ROW, ROW)], scratch[bass.ds(first, P), :]).then_inc(xs_in, 16)

            load_slot(0)
            with sp.Fori(1, SLOTS) as s:
                load_slot(s)

        def tiles(b):
            return (HALVES * b, HALVES, P) if b < B else (CLS, 1, B)

        @block.gpsimd
        def _(pool):
            def gather(dst, src, col, signal):
                pool.indirect_dma_start(
                    out=dst, out_offset=None, in_=src,
                    in_offset=bass.IndirectOffsetOnAxis(ap=idx_sb[:, col:col + 1].bitcast(U32), axis=0),
                ).then_inc(signal, 16)

            def inverse_deviation(dst, var, n, signal):
                pool.tensor_tensor(dst, var, half_neg[:, 0:n][0:dst.shape[0]], ALU.pow).then_inc(signal, 1)

            pool.wait_ge(idx_in, 16)
            for g in range(GP // G2):
                gather(px2[:, g, :], pix2, g, px2_in)
            for g in range(GP // G1):
                gather(px1[:, g, :], pix1, COL1 + g, px1_in)
            pool.wait_ge(prep, 2)
            pool.wait_ge(var1_ready, 1)
            inverse_deviation(rstd1[0:B, CLS:TILES], mv1[0:B, CLS, 1:2], 1, rstd1_ready)
            for g in range(GP):
                gather(px0[:, g, :], pix0, COL0 + g, px0_in[0])
            for g in range(GP):
                if g == 13:
                    pool.wait_ge(var1_ready, 2)
                    inverse_deviation(rstd1[:, 0:B], mv1[:, 0:B, 1], B, rstd1_ready)
                gather(px0[:, GP + g, :], pix0, COL0 + GP + g, px0_in[1])
            pool.iota(rows_i[:, 0:CLS, C + 3], [[S, B], [P, HALVES]], base=1,
                      channel_multiplier=1).then_inc(row_ids, 1)
            pool.iota(rows_i[0:B, CLS, C + 3:C + 4], [[0, 1]], base=0, channel_multiplier=S).then_inc(row_ids, 1)
            pool.wait_ge(var1_ready, 3)
            inverse_deviation(rstd1[:, B:2 * B], mv1[:, B:2 * B, 1], B, rstd1_ready)

            def scatter(t, n):
                pool.indirect_dma_start(
                    out=scratch, out_offset=bass.IndirectOffsetOnAxis(ap=pos_i[0:n, t:t + 1].bitcast(U32), axis=0),
                    in_=rows[0:n, t, :], in_offset=None).then_inc(row_out, 16)

            def row_deviations(b):
                pool.wait_ge(var2_ready, b + 1)
                t, n, m = tiles(b)
                inverse_deviation(rows[0:m, t:t + n, C + 1], vare[0:m, t:t + n], n, rstd2_ready)

            def send_rows(b):
                t, n, m = tiles(b)
                pool.wait_ge(pos_ready, b + 1)
                pool.wait_ge(rstd2_ready, b + 1)
                pool.wait_ge(row_ids, 2)
                if b == 0:
                    pool.wait_ge(empty_out, 16 * (E + 1))
                for i in range(n):
                    scatter(t + i, m)

            def spread_queries(n):
                b, g = divmod(n, G)
                pool.wait_ge(q_in, n + 1)
                if b >= 2:
                    pool.wait_ge(sc_mm, H * (b - 1))
                for h in range(HG):
                    pool.tensor_scalar(q_head[:, b % 2, g, h, :], q_sb[:, 0:N], k[0:GH, K_MQ + h:K_MQ + h + 1], None,
                                       ALU.mult).then_inc(q_ev, 1)

            work = {"q": spread_queries, "pj": row_deviations, "rk": send_rows}
            for kind, n in FIRST + sum(PLAN, []):
                if kind in work:
                    work[kind](n)

            for s in range(SLOTS):
                pool.wait_ge(y_ready, s + 1)
                pool.indirect_dma_start(out=out, out_offset=bass.IndirectOffsetOnAxis(ap=y_row[:, 0:1], axis=0),
                                        in_=y[:, :], in_offset=None, bounds_check=B * S - 1,
                                        oob_is_err=False).then_inc(y_out, 16)
            pool.wait_ge(y_out, 16 * SLOTS)

        def probs_in(eng, hh):
            eng.wait_ge(pt_dve, (hh + 2) // 2)
            if hh >= 1:
                eng.wait_ge(pt_act, (hh + 1) // 2)

        @block.tensor
        def _(pe):
            def mm(dst, lhs, rhs, first, last):
                return pe.matmul(dst, lhs, rhs, start=first, stop=last)

            pe.wait_ge(lw_in, 16)
            pe.wait_ge(wft_in, 16)
            rounds = [[(0, L0, 0)], [(L0 + (L1 // G1) * g, L1 // G1, 1) for g in range(G1)]]
            rounds += [[(L0 + L1 + (L2 // G2) * g, L2 // G2, 2) for g in (j, j + 1)] for j in range(0, G2, 2)]
            for r, work in enumerate(rounds):
                if r >= 2:
                    pe.wait_ge(cw_ev, r - 1)
                for i, (at, m, level) in enumerate(work):
                    last = mm(bank[MISC[r % 2]][0:m, i * C:(i + 1) * C], lw_sb[:, at:at + m], wft_sb[:, level, :],
                              True, True)
                last.then_inc(cw_mm, 1)

            pe.wait_ge(k_in, 16)
            pe.wait_ge(clsn, 1)
            for t in range(2):
                last = pe.transpose(bank[5][0:KH, t * B:(t + 1) * B], xn1c[:, t:C:2], ident[0:B, 0:B])
            last.then_inc(cls_t, 1)
            pe.wait_ge(cls_ev, 1)
            pe.wait_ge(prep, 4)
            for g in range(G):
                for t in range(2):
                    last = mm(bank[4][:, g * B:(g + 1) * B],
                              wv_pad[:, t, g * HG:(g + 1) * HG, :].rearrange("p h d -> p (h d)"),
                              xt1[:, t, :, N], t == 0, t == 1)
            last.then_inc(vcls_mm, 1)

            pe.wait_ge(px2_by_image, 1)
            for b in range(B):
                last = pe.transpose(bank[5][0:L2 // G2, b * P:(b + 1) * P], px2b[:, b, :], ident)
            last.then_inc(px2_t, 1)
            pe.wait_ge(px2_ev, 1)
            pe.wait_ge(cw_ev, len(rounds))
            pe.wait_ge(vcls_ev, 1)
            pe.wait_ge(lb_ready, 1)
            pe.wait_ge(small_in, 16 * 3)
            f2_ps = bank[4][EMB:P, 0:C]
            for g in range(G2):
                mm(f2_ps, px2t[:, g, :, :].rearrange("p b m -> p (b m)"), c2[:, g, :], g == 0, False)
            for level in range(3):
                mm(f2_ps, lb_rep[:, level, :], wft_sb[:, level, :], False, False)
            mm(f2_ps, k[0:1, K_ONE:K_ONE + B * N2], bf_sb[:, :], False, True).then_inc(f2_mm, 1)

            pe.wait_ge(px1_by_image, 1)
            for b in range(B):
                last = pe.transpose(bank[5][0:L1 // G1, b * P:(b + 1) * P], px1b[:, b, :], ident)
            last.then_inc(px1_t, 1)
            pe.wait_ge(px1_ev, 1)
            pe.wait_ge(f2_ev, 1)
            for pair in range(2):
                for g in range(G1):
                    last = mm(bank[4][:, pair * C:(pair + 1) * C],
                              px1t[:, g, 2 * pair:2 * pair + 2, :].rearrange("p b m -> p (b m)"), c1[:, g, :],
                              g == 0, g == G1 - 1)
            last.then_inc(f1_mm, 1)

            for half in range(HALVES):
                pe.wait_ge(px0_by_image, half + 1)
                if half:
                    pe.wait_ge(v_ev, B)
                for b in range(B):
                    last = pe.transpose(bank[5][0:L0, b * P:(b + 1) * P],
                                        px0b[:, b, :], ident)
                last.then_inc(px0_t, 1)
                pe.wait_ge(px0_ev, half + 1)
                if half == 0:
                    pe.wait_ge(int2_in, 16)
                    pe.wait_ge(f1_ev, 1)
                for b in range(B):
                    if half:
                        pe.wait_ge(xn1_ready, b + 1)
                    mm(bank[b][:, 0:C], tok_l[:, b, half, :], tok_r[:, :], True, False)
                    at = K_I1 + ((b % 2) * HALVES + half) * P
                    mm(bank[b][:, 0:C], k[:, at:at + P], f1[:, b // 2, :], False, True).then_inc(tok_mm, 1)
                for b in range(B + 1):
                    n = half * B + b
                    if b < B:
                        pe.wait_ge(xn1_ready, n + 1)
                        if n >= 2:
                            pe.wait_ge(xt1_ev, n - 1)
                        for t in range(2):
                            last = pe.transpose(bank[MISC[b % 2]][0:KH, t * P:(t + 1) * P], xn1[:, b, t:C:2], ident)
                        last.then_inc(xt1_t, 1)
                    if b == 0:
                        continue
                    b, n = b - 1, n - 1
                    pe.wait_ge(xt1_ev, n + 1)
                    if n >= 2:
                        pe.wait_ge(v_ev, n - 1)
                    for t in range(2):
                        last = mm(bank[4 + b % 2][:, 0:C], xt1[:, t, b, half * P:(half + 1) * P],
                                  wqkv_sb[:, t, 2 * C:3 * C], t == 0, t == 1)
                    last.then_inc(v_mm, 1)

            def queries_or_keys(kind, n, dst):
                b, g = divmod(n, G)
                at = (0 if kind == "q" else C) + g * GH
                for t in range(2):
                    last = mm(dst[0:GH, 0:S], wqkv_sb[:, t, at:at + GH], xt1[:, t, b, :], t == 0, t == 1)
                last.then_inc(q_mm if kind == "q" else k_mm, 1)

            def class_scores(b, dst):
                pe.wait_ge(qc_ev, G * (b + 1))
                pe.wait_ge(k_ev, G * (b + 1))
                for g in range(G):
                    last = mm(dst[0:H, 0:S], q_cls[:, b % 2, g, :], k_sb[:, b % 2, g, :], g == 0, g == G - 1)
                last.then_inc(csc_mm, 1)

            def class_turn(b, dst):
                pe.wait_ge(crp_ready, b + 1)
                for i in range(HALVES):
                    pe.transpose(dst[:, i * H:(i + 1) * H], probs_c[:, i * P:(i + 1) * P], ident[0:H, 0:H])
                for g in range(G):
                    last = mm(dst[:, 32 + 2 * g:34 + 2 * g], k[0:H, K_SEL + g * P:K_SEL + (g + 1) * P], rp_c[:, :],
                              True, True)
                last.then_inc(cp_t, 1)

            def scores(hh):
                b, h = divmod(hh, H)
                pe.wait_ge(q_ev, hh + 1)
                if h % HG == 0:
                    pe.wait_ge(k_ev, hh // HG + 1)
                if hh >= 2:
                    pe.wait_ge(exp_ready, 2 * (hh - 1))
                for i in range(HALVES):
                    last = mm(bank[2 * (hh % 2) + i][:, 0:S], q_head[:, b % 2, h // HG, h % HG, i * P:(i + 1) * P],
                              k_sb[:, b % 2, h // HG, :], True, True)
                last.then_inc(sc_mm, 1)

            def turn_probs(hh):
                h = hh % H
                pe.wait_ge(exp_ready, 2 * (hh + 1))
                if hh:
                    probs_in(pe, hh - 1)
                for i in range(HALVES):
                    for j in range(HALVES):
                        last = pe.transpose(bank[5][:, (j * HALVES + i) * P:(j * HALVES + i + 1) * P],
                                            probs[:, h, i, j * P:(j + 1) * P], ident)
                last.then_inc(p_t, 1)

            def values(n):
                b, g = divmod(n, G)
                probs_in(pe, HG * (n + 1) - 1)
                if g == 0:
                    pe.wait_ge(col_ready, b + 1)
                if n:
                    pe.wait_ge(part_ready, n)
                for j in range(HALVES):
                    for q in range(HG):
                        h = g * HG + q
                        last = mm(bank[4][q * HP:(q + 1) * HP, 0:S], v_sb[:, b, j, h, :], pt[:, h, j, :],
                                  j == 0, j == HALVES - 1)
                last.then_inc(pv_mm, 1)

            def factors(n, dst):
                pe.wait_ge(rp_rows_ready, n + 1)
                for w in range(2):
                    for i in range(HALVES):
                        at = (w * HALVES + i) * P
                        last = pe.transpose(dst[:, at:at + P], rp_rows[:, w, i, :], ident)
                last.then_inc(rp_t, 1)

            def project(b, dst):
                if b < B:
                    pe.wait_ge(ot_ready, G * (b + 1))
                n = HALVES if b < B else 1
                for i in range(n):
                    for g in range(G):
                        lhs, m = (ot[:, b, g, i * P:(i + 1) * P], P) if b < B else (ot[:, :, g, N], B)
                        last = mm(dst[0:m, i * C:(i + 1) * C], lhs, wproj_sb[:, g, :], g == 0, g == G - 1)
                last.then_inc(proj_mm, 1)

            def turn_rows(b, dst):
                _, n, m = tiles(b)
                pe.wait_ge(xn2_ready, b + 1)
                for i in range(n):
                    for t in range(2):
                        last = pe.transpose(dst[0:KH, (i * 2 + t) * P:(i * 2 + t) * P + m], xn2[0:m, i, t:C:2],
                                            ident[0:m, 0:m])
                last.then_inc(xt2_t, 1)

            def route(b, dst):
                _, n, m = tiles(b)
                pe.wait_ge(xt2_ev, b + 1)
                for i in range(n):
                    for t in range(2):
                        last = mm(dst[0:m, i * E:(i + 1) * E], xt2[:, i, t, 0:m], rw_sb[:, t, :], t == 0, t == 1)
                last.then_inc(lg_mm, 1)

            def rank(b, dst):
                t0, n, m = tiles(b)
                pe.wait_ge(chosen_ready, b + 1)
                for i in range(n):
                    for before in range(t0 + i):
                        mm(dst[0:m, i * E:(i + 1) * E], one_bf[:, 0:m], chosen[:, before, :], before == 0, False)
                    last = mm(dst[0:m, i * E:(i + 1) * E], tri_bf[0:m, 0:m], chosen[0:m, t0 + i, :], t0 + i == 0, True)
                last.then_inc(rank_mm, 1)

            def count(_, dst):
                for t in range(TILES):
                    m = P if t < CLS else B
                    last = mm(dst[0:1, 0:E], one_bf[0:m, 0:1], chosen[0:m, t, :], t == 0, t == TILES - 1)
                last.then_inc(cnt_mm, 1)

            work = {
                "q": (lambda n, dst: queries_or_keys("q", n, dst), q_in), "k": (lambda n, dst: queries_or_keys("k", n, dst), k_ev),
                "cs": (class_scores, cexp_ready), "ct": (class_turn, cp_ev), "f": (factors, rp_ev),
                "pj": (project, h2_ready), "xr": (turn_rows, xt2_ev), "lg": (route, lg_ready), "rk": (rank, place_ready),
                "cn": (count, slots_ready),
            }
            last_turns = []

            def spare(kind, n):
                if len(last_turns) >= 2:
                    before, m = last_turns[-2]
                    pe.wait_ge(work[before][1], m + 1)
                last_turns.append((kind, n))
                work[kind][0](n, SPARE[kind, n])

            pe.wait_ge(rout_w_in, 16 * 2)
            pe.wait_ge(attn_w_in, 16 * 2)
            pe.wait_ge(consts_bf, 2)
            pe.wait_ge(v_ev, 2 * B)
            for task in FIRST:
                spare(*task)
            for hh in range(len(PLAN)):
                if hh < HEADS:
                    scores(hh)
                if TURN_LAG <= hh < HEADS + TURN_LAG:
                    turn_probs(hh - TURN_LAG)
                if hh >= VALUES_LAG and (hh - VALUES_LAG) % HG == 0:
                    values((hh - VALUES_LAG) // HG)
                for task in PLAN[hh]:
                    spare(*task)

            def slot_turn(s):
                pe.wait_ge(xn3_ready, s + 1)
                for t in range(2):
                    last = pe.transpose(bank[2][0:KH, t * P:(t + 1) * P], xn3[:, t:C:2], ident)
                last.then_inc(xt3_t, 1)

            def slot_up(s):
                e = pe.value_load(slot_i[0:1, 0, bass.ds(s, 1)], min_val=0, max_val=E - 1)
                pe.wait_ge(xt3_ev, s + 1)
                for i in range(2):
                    for t in range(2):
                        last = mm(bank[i][:, :], xt3[:, t, :],
                                  w12_sb[:, bass.ds(e * (4 * HID) + (i * 2 + t) * HID, HID)], t == 0, t == 1)
                last.then_inc(up_mm, 1)

            def slot_down(s):
                e = pe.value_load(slot_i[0:1, 0, bass.ds(s, 1)], min_val=0, max_val=E - 1)
                pe.wait_ge(hid_t_ev, s + 1)
                after_slots(pe, obf_ready, s)
                for c in range(HC):
                    last = mm(bank[4][:, 0:C], hid_t[:, c, :], w3_sb[:, bass.ds(e * (HC * C) + c * C, C)],
                              c == 0, c == HC - 1)
                last.then_inc(down_mm, 1)

            def slot_turn_hidden(s):
                pe.wait_ge(hid_ready, s + 1)
                for c in range(HC):
                    last = pe.transpose(bank[3][:, c * P:(c + 1) * P], hid[:, c:HID:HC], ident)
                last.then_inc(hid_t_t, 1)

            pe.wait_ge(slots_ready, 1)
            for e in range(E):
                pe.wait_ge(w_in[e], 16 * 3)
            slot_turn(0)
            slot_up(0)
            slot_turn(1)
            slot_turn_hidden(0)

            def slot_step(s):
                slot_up(s)
                slot_turn(s + 1)
                slot_down(s - 1)
                slot_turn_hidden(s)

            slot_step(1)
            with pe.Fori(0, (SLOTS - 3) // STEPS) as turn:
                for step in range(STEPS):
                    slot_step(turn * STEPS + 2 + step)
            slot_up(SLOTS - 1)
            slot_down(SLOTS - 2)
            slot_turn_hidden(SLOTS - 1)
            slot_down(SLOTS - 1)

        @block.scalar
        def _(act):
            act.dma_start(k[:, :], consts).then_inc(k_in, 16)
            act.dma_start(cls_x[:, :], cls_tok.broadcast_to([B, C])).then_inc(small_in, 16)
            act.dma_start(bf_sb[:, :], bf).then_inc(small_in, 16)
            act.dma_start(lb_sb[:, :], lb).then_inc(small_in, 16)
            act.dma_start(bproj_sb[:, :], bproj.broadcast_to([P, C])).then_inc(attn_w_in, 16)

            def copy(dst, src):
                return act.activation(dst, src, ACT.Copy)

            act.wait_ge(prep, 1)
            act.wait_ge(cw_mm, 1)
            copy(tok_r[0:L0, :], bank[MISC[0]][0:L0, 0:C]).then_inc(cw_ev, 1)
            act.wait_ge(cw_mm, 2)
            copy(c1[:, :, :], bank[MISC[1]][0:L1 // G1, 0:2 * C].rearrange("p (g c) -> p g c", g=2)).then_inc(cw_ev, 1)
            for j in range(G2 // 2):
                act.wait_ge(cw_mm, 3 + j)
                copy(c2[:, 2 * j:2 * j + 2, :],
                     bank[MISC[j % 2]][0:L2 // G2, 0:2 * C].rearrange("p (g c) -> p g c", g=2)).then_inc(cw_ev, 1)
            act.wait_ge(f2_mm, 1)
            copy(tok_r[EMB:P, :], bank[4][EMB:P, 0:C]).then_inc(f2_ev, 1)
            act.wait_ge(f1_mm, 1)
            copy(f1[:, :, :], bank[4][:, 0:2 * C].rearrange("p (g c) -> p g c", g=2)).then_inc(f1_ev, 1)

            act.wait_ge(prep, 5)
            def rows_turned(half, b):
                act.wait_ge(xt1_t, half * B + b + 1)
                copy(xt1[:, :, b, half * P:(half + 1) * P],
                     bank[MISC[b % 2]][0:KH, 0:2 * P].rearrange("p (t n) -> p t n", t=2)).then_inc(xt1_ev, 1)

            def values_made(half, b):
                act.wait_ge(v_mm, half * B + b + 1)
                copy(v_sb[:, b, half, :, 0:D],
                     bank[4 + b % 2][:, 0:C].rearrange("p (h d) -> p h d", h=H)).then_inc(v_ev, 1)

            for half in range(HALVES):
                rows_turned(half, 0)
                for b in range(1, B):
                    rows_turned(half, b)
                    values_made(half, b - 1)
                values_made(half, B - 1)

            def queries(n, src):
                act.wait_ge(q_mm, n + 1)
                if n:
                    act.wait_ge(q_ev, HG * n)
                    act.wait_ge(qc_ev, n)
                act.activation(q_sb[:, :], src[0:GH, 0:S], ACT.Copy, scale=SCALE).then_inc(q_in, 1)

            def exps(hh):
                h = hh % H
                act.wait_ge(max_ready, hh + 1)
                if hh >= H:
                    act.wait_ge(p_t, hh - H + 1)
                    act.wait_ge(rp_ready, hh // HG - 1)
                for i in range(HALVES):
                    act.activation(probs[:, h, i, :], bank[2 * (hh % 2) + i][:, 0:S], ACT.Exp,
                                   bias=nmax[:, h, i:i + 1], accum_out=den[:, h, i:i + 1]).then_inc(exp_ready, 1)

            def turned_probs(hh):
                h = hh % H
                act.wait_ge(p_t, hh + 1)
                if hh >= H:
                    act.wait_ge(pv_mm, hh // HG - G + 1)
                copy(pt[:, h, :, 0:N], bank[5][:, :].rearrange("p (j n) -> p j n", j=2)).then_inc(pt_act, 1)

            def class_exps(b, src):
                act.wait_ge(cmax_ready, b + 1)
                if b:
                    act.wait_ge(cp_t, b)
                act.activation(probs_c[:, :], src[0:H, 0:S], ACT.Exp, bias=nmax_c[:, :],
                               accum_out=den_c[:, :]).then_inc(cexp_ready, 1)

            def factors(n, src):
                act.wait_ge(rp_t, n + 1)
                if n:
                    act.wait_ge(ot_ready, n)
                copy(rpt[:, :, 0:N], src[:, :].rearrange("p (w n) -> p w n", w=2)).then_inc(rp_ev, 1)

            def turned_rows(b, src):
                _, n, m = tiles(b)
                act.wait_ge(xt2_t, b + 1)
                if b:
                    act.wait_ge(lg_mm, b)
                src = src[0:KH, :].rearrange("p (i t n) -> p i t n", i=2, t=2)
                copy(xt2[:, 0:n, :, 0:m], src[:, 0:n, :, 0:m]).then_inc(xt2_ev, 1)

            def route_exps(b, _):
                _, n, m = tiles(b)
                act.wait_ge(ntop_ready, b + 1)
                if b:
                    act.wait_ge(prob_ready, b)
                for i in range(n):
                    act.activation(prob_e[0:m, i, :], logits[0:m, i, :], ACT.Exp, bias=ntop[0:m, i:i + 1],
                                   accum_out=prob_s[0:m, i:i + 1]).then_inc(pexp_ready, 1)

            work = {"q": queries, "cs": class_exps, "f": factors, "xr": turned_rows, "rk": route_exps}

            def tasks(plan):
                for kind, n in plan:
                    if kind in work:
                        work[kind](n, SPARE[kind, n])

            act.wait_ge(k_in, 16)
            tasks(FIRST)
            for hh in range(len(PLAN)):
                if hh < HEADS:
                    exps(hh)
                if TURN_LAG <= hh < HEADS + TURN_LAG and hh % 2 == 1:
                    turned_probs(hh - TURN_LAG)
                tasks(PLAN[hh])

            def slot_turned(s):
                act.wait_ge(xt3_t, s + 1)
                copy(xt3[:, :, :], bank[2][0:KH, 0:2 * P].rearrange("p (t n) -> p t n", t=2)).then_inc(xt3_ev, 1)

            def slot_gate(s):
                act.wait_ge(up_mm, s + 1)
                act.activation(gate[:, :], bank[0][:, :], ACT.Silu).then_inc(gate_ready, 1)

            def slot_result(s):
                act.wait_ge(down_mm, s + 1)
                after_slots(act, y_ready, s)
                copy(o_bf[:, :], bank[4][:, 0:C]).then_inc(obf_ready, 1)

            def slot_turned_hidden(s):
                act.wait_ge(hid_t_t, s + 1)
                copy(hid_t[:, :, :], bank[3][:, :].rearrange("p (c n) -> p c n", c=HC)).then_inc(hid_t_ev, 1)

            slot_turned(0)
            slot_gate(0)
            slot_turned(1)
            slot_turned_hidden(0)

            def slot_step(s):
                slot_gate(s)
                slot_turned(s + 1)
                slot_result(s - 1)
                slot_turned_hidden(s)

            slot_step(1)
            with act.Fori(0, (SLOTS - 3) // STEPS) as turn:
                for step in range(STEPS):
                    slot_step(turn * STEPS + 2 + step)
            slot_gate(SLOTS - 1)
            slot_result(SLOTS - 2)
            slot_turned_hidden(SLOTS - 1)
            slot_result(SLOTS - 1)

        @block.vector
        def _(dve):
            done = [0]

            def then(ins):
                done[0] += 1
                ins.then_inc(dve_done, 1)
                dve.wait_ge(dve_done, done[0])

            dve.memset(tok_r[:, :], 0.0).then_inc(prep, 1)
            dve.memset(half_neg[:, :], -0.5).then_inc(prep, 1)
            then(dve.memset(empty[:, :, :], 0.0))
            dve.memset(empty[:, :, C + 3:C + 4].bitcast(I32), NO_ROW).then_inc(empty_ready, 1)
            then(dve.memset(wv_pad[:, :, :, :], 0.0))
            dve.wait_ge(wqkv_in, 16)
            dve.memset(nmax[:, :, :], 0.0).then_inc(prep, 1)
            dve.tensor_copy(wv_pad[:, :, :, 0:D],
                            wqkv_sb[:, :, 2 * C:3 * C].rearrange("p t (h d) -> p t h d", h=H)).then_inc(prep, 1)
            dve.memset(v_sb[:, :, :, :, :], 0.0).then_inc(prep, 1)
            dve.wait_ge(k_in, 16)
            dve.tensor_copy(tri_bf[:, :], k[:, K_TRI:K_TRI + P]).then_inc(consts_bf, 1)
            dve.tensor_copy(one_bf[:, :], k[:, K_ONE:K_ONE + P]).then_inc(consts_bf, 1)
            dve.wait_ge(small_in, 16 * 3)
            dve.tensor_copy(lb_rep[:, :, :], lb_sb[:, :].unsqueeze(2).broadcast_to([EMB, 3, B * N2])).then_inc(lb_ready, 1)
            dve.wait_ge(attn_w_in, 16 * 2)

            def residual(tile, t, m, src):
                dve.tensor_tensor(h1[0:m, tile, :], src, bproj_sb[0:m, :], ALU.add).then_inc(h1_ready, 1)
                then(dve.bn_stats(stat1[0:m, t, :], src))
                then(dve.bn_aggr(mv1[0:m, t, :], stat1[0:m, t, :]))

            def plus_eps(t, n, m):
                dve.tensor_scalar(mv1[0:m, t:t + n, 1], mv1[0:m, t:t + n, 1], EPS, None, ALU.add).then_inc(var1_ready, 1)

            def by_image(dst, src, signal):
                dve.tensor_copy(dst.rearrange("p b (g v) -> p g b v", g=src.shape[1]),
                                src.rearrange("p g (b v) -> p g b v", b=B)).then_inc(signal, 1)

            def turned(dst, groups, rows_n, wait, signal):
                dve.wait_ge(wait, 1)
                dve.tensor_copy(dst.rearrange("p g b m -> p b g m"),
                                bank[5][0:rows_n, :].rearrange("p (b g m) -> p b g m", b=B, g=groups)).then_inc(signal, 1)

            residual(CLS, CLS, B, cls_x[:, :])
            plus_eps(CLS, 1, B)
            dve.wait_ge(rstd1_ready, 1)
            dve.tensor_scalar(xn1c[:, :], cls_x[:, :], mv1[0:B, CLS, 0:1], rstd1[0:B, CLS:TILES], ALU.subtract,
                              ALU.mult).then_inc(clsn, 1)
            dve.wait_ge(cls_t, 1)
            dve.tensor_copy(xt1[:, :, :, N], bank[5][0:KH, 0:2 * B].rearrange("p (t b) -> p t b", t=2)).then_inc(cls_ev, 1)
            dve.wait_ge(vcls_mm, 1)
            dve.tensor_copy(vcls[:, :, :], bank[4][:, 0:G * B].rearrange("p (g b) -> p g b", g=G)).then_inc(vcls_ev, 1)

            dve.wait_ge(px2_in, 16 * (GP // G2))
            by_image(px2b[:, :, :], px2[:, :, :], px2_by_image)
            turned(px2t[:, :, :, :], G2, L2 // G2, px2_t, px2_ev)
            dve.wait_ge(px1_in, 16 * (GP // G1))
            by_image(px1b[:, :, :], px1[:, :, :], px1_by_image)
            turned(px1t[:, :, :, :], G1, L1 // G1, px1_t, px1_ev)
            for half in range(HALVES):
                dve.wait_ge(px0_in[half], 16 * GP)
                if half:
                    dve.wait_ge(px0_t, half)
                by_image(px0b[:, :, :], px0[:, half * GP:(half + 1) * GP, :], px0_by_image)
                dve.wait_ge(px0_t, half + 1)
                dve.tensor_copy(tok_l[0:L0, :, half, :],
                                bank[5][0:L0, :].rearrange("p (b n) -> p b n", b=B)).then_inc(px0_ev, 1)
                for b in range(B):
                    dve.wait_ge(tok_mm, half * B + b + 1)
                    residual(HALVES * b + half, half * B + b, P, bank[b][:, 0:C])
                plus_eps(half * B, B, P)
                dve.wait_ge(rstd1_ready, half + 2)
                for b in range(B):
                    t = half * B + b
                    if half:
                        dve.wait_ge(xt1_t, b + 1)
                    dve.tensor_scalar(xn1[:, b, :], bank[b][:, 0:C], mv1[:, t, 0:1], rstd1[:, t:t + 1], ALU.subtract,
                                      ALU.mult).then_inc(xn1_ready, 1)

            def class_query(n, _):
                b, g = divmod(n, G)
                dve.wait_ge(q_in, n + 1)
                if b >= 2:
                    dve.wait_ge(csc_mm, b - 1)
                dve.tensor_scalar(q_cls[:, b % 2, g, :], k[0:GH, K_M8 + g * H:K_M8 + (g + 1) * H], q_sb[:, N:S],
                                  None, ALU.mult).then_inc(qc_ev, 1)

            def keys(n, src):
                b, g = divmod(n, G)
                dve.wait_ge(k_mm, n + 1)
                if b >= 2:
                    dve.wait_ge(sc_mm, H * (b - 1))
                    dve.wait_ge(csc_mm, b - 1)
                dve.tensor_copy(k_sb[:, b % 2, g, :], src[0:GH, 0:S]).then_inc(k_ev, 1)

            def class_max(b, src):
                dve.wait_ge(csc_mm, b + 1)
                if b:
                    dve.wait_ge(cexp_ready, b)
                dve.tensor_reduce(nmax_c[:, :], src[0:H, 0:S], AX_X, ALU.max, negate=True).then_inc(cmax_ready, 1)

            def class_factors(b):
                dve.wait_ge(cexp_ready, b + 1)
                if b:
                    dve.wait_ge(cp_t, b)
                then(dve.reciprocal(rp_c[:, 0:1], den_c[:, :]))
                dve.tensor_scalar(rp_c[:, 1:2], probs_c[:, N:S], rp_c[:, 0:1], None, ALU.mult).then_inc(crp_ready, 1)

            def class_turned(b, src):
                dve.wait_ge(cp_t, b + 1)
                dve.tensor_copy(rpc[:, b % 2, :, :],
                                src[:, 32:32 + 2 * G].rearrange("p (g w) -> p g w", g=G)).then_inc(rpc_ready, 1)
                if b:
                    dve.wait_ge(col_ready, b)
                dve.tensor_copy(col[:, :, :], src[:, 0:HALVES * H].rearrange("p (j h) -> p j h", j=HALVES))\
                   .then_inc(cp_ev, 1)

            def class_columns(b):
                dve.wait_ge(cp_ev, b + 1)
                if b:
                    dve.wait_ge(pv_mm, G * b)
                dve.tensor_copy(pt[:, :, :, N].rearrange("p h j -> p j h"), col[:, :, :]).then_inc(col_ready, 1)

            def maxes(hh):
                h = hh % H
                dve.wait_ge(sc_mm, hh + 1)
                if hh >= H:
                    dve.wait_ge(exp_ready, 2 * (hh - H + 1))
                at = 2 * (hh % 2)
                dve.tensor_reduce(nmax[:, h, :], psum[:, at:at + HALVES, 0:S], AX_X, ALU.max, negate=True)\
                   .then_inc(max_ready, 1)

            def turned_probs(hh):
                h = hh % H
                dve.wait_ge(p_t, hh + 1)
                if hh >= H:
                    dve.wait_ge(pv_mm, hh // HG - G + 1)
                dve.tensor_copy(pt[:, h, :, 0:N], bank[5][:, :].rearrange("p (j n) -> p j n", j=2)).then_inc(pt_dve, 1)

            def ratios(n):
                g = n % G
                heads = slice(g * HG, (g + 1) * HG)
                dve.wait_ge(exp_ready, 2 * HG * (n + 1))
                if n:
                    dve.wait_ge(rp_t, n)
                then(dve.reciprocal(rp[:, 0, :, heads], den[:, heads, :].rearrange("p h i -> p i h")))
                dve.tensor_tensor(rp[:, 1, :, heads], rp[:, 0, :, heads],
                                  probs[:, heads, :, N].rearrange("p h i -> p i h"), ALU.mult).then_inc(rp_ready, 1)
                dve.wait_ge(rp_ready, n + 1)
                dve.tensor_copy(rp_rows[:, :, :, :].rearrange("p w i (h d) -> p (w i) h d", h=HG),
                                rp[:, :, :, heads].rearrange("p w i h -> p (w i) h").unsqueeze(3)
                                .broadcast_to([P, 2 * HALVES, HG, HP])).then_inc(rp_rows_ready, 1)

            def finish_group(n):
                b, g = divmod(n, G)
                dve.wait_ge(rp_ev, n + 1)
                dve.wait_ge(rpc_ready, b + 1)
                then(dve.tensor_copy(rpt[:, :, N], rpc[:, b % 2, g, :]))
                dve.wait_ge(pv_mm, n + 1)
                if n:
                    dve.wait_ge(ot_ready, n)
                dve.tensor_tensor(part[:, :], bank[4][:, 0:S], rpt[:, 0, :], ALU.mult).then_inc(part_ready, 1)
                dve.wait_ge(part_ready, n + 1)
                dve.scalar_tensor_tensor(out=ot[:, b, g, :], in0=rpt[:, 1, :], scalar=vcls[:, g, b:b + 1],
                                         in1=part[:, :], op0=ALU.mult, op1=ALU.add).then_inc(ot_ready, 1)

            def second_residual(b, src):
                t, n, m = tiles(b)
                dve.wait_ge(proj_mm, b + 1)
                dve.tensor_tensor(rows[0:m, t:t + n, 0:C], src[0:m, 0:n * C].rearrange("p (i c) -> p i c", i=n),
                                  h1[0:m, t:t + n, :], ALU.add).then_inc(h2_ready, 1)
                dve.wait_ge(h2_ready, b + 1)
                for i in range(n):
                    then(dve.bn_stats(stat2[0:m, i, :], rows[0:m, t + i, 0:C]))
                    then(dve.bn_aggr(rows[0:m, t + i, C:C + 2], stat2[0:m, i, :]))
                dve.tensor_scalar(vare[0:m, t:t + n], rows[0:m, t:t + n, C + 1], EPS, None, ALU.add)\
                   .then_inc(var2_ready, 1)

            def second_norm(b):
                t, n, m = tiles(b)
                dve.wait_ge(rstd2_ready, b + 1)
                if b:
                    dve.wait_ge(xt2_t, b)
                for i in range(n):
                    last = dve.tensor_scalar(xn2[0:m, i, :], rows[0:m, t + i, 0:C], rows[0:m, t + i, C:C + 1],
                                             rows[0:m, t + i, C + 1:C + 2], ALU.subtract, ALU.mult)
                last.then_inc(xn2_ready, 1)

            def choose(b, src):
                t, n, m = tiles(b)
                dve.wait_ge(lg_mm, b + 1)
                if b:
                    dve.wait_ge(pexp_ready, HALVES * b)
                dve.tensor_tensor(logits[0:m, 0:n, :], src[0:m, 0:n * E].rearrange("p (i e) -> p i e", i=n),
                                  rb_sb[0:m, :].unsqueeze(1).broadcast_to([m, n, E]), ALU.add).then_inc(lg_ready, 1)
                dve.wait_ge(lg_ready, b + 1)
                for i in range(n):
                    last = dve.max(top[0:m, i, :], logits[0:m, i, :])
                then(last)
                dve.tensor_scalar(ntop[0:m, 0:n], top[0:m, 0:n, 0], -1.0, None, ALU.mult).then_inc(ntop_ready, 1)
                for i in range(n):
                    last = dve.max_index(topi[0:m, i, :], top[0:m, i, :], logits[0:m, i, :])
                then(last)
                for i in range(n):
                    last = dve.tensor_scalar(chosen[0:m, t + i, :], k[0:m, K_E:K_E + E], topi[0:m, i, 0:1], None,
                                             ALU.is_equal)
                last.then_inc(chosen_ready, 1)

            def place_rows(b, src):
                t, n, m = tiles(b)
                dve.wait_ge(rank_mm, b + 1)
                dve.tensor_tensor(place[0:m, 0:n, :], src[0:m, 0:n * E].rearrange("p (i e) -> p i e", i=n),
                                  k[0:m, K_BASE:K_BASE + E].unsqueeze(1).broadcast_to([m, n, E]),
                                  ALU.add).then_inc(place_ready, 1)
                dve.wait_ge(place_ready, b + 1)
                then(dve.tensor_tensor(place2[0:m, 0:n, :], place[0:m, 0:n, :], chosen[0:m, t:t + n, :], ALU.mult))
                then(dve.tensor_reduce(pos[0:m, t:t + n], place2[0:m, 0:n, :], AX_X, ALU.add))
                dve.wait_ge(pexp_ready, min(HALVES * (b + 1), TILES))
                dve.reciprocal(rows[0:m, t:t + n, C + 2], prob_s[0:m, 0:n]).then_inc(prob_ready, 1)
                dve.tensor_copy(pos_i[0:m, t:t + n], pos[0:m, t:t + n]).then_inc(pos_ready, 1)

            def fill_slots(_, src):
                dve.wait_ge(cnt_mm, 1)
                one = k[0:1, :]

                def grid(at, a, c):
                    return one[:, at:at + a * c].rearrange("p (a c) -> p a c", a=a)

                over = nt[:, 0:E * NJ].rearrange("p (a c) -> p a c", a=E)
                n_slots, step, end = (nt[:, E * NJ + i * E:E * NJ + (i + 1) * E] for i in range(3))
                then(dve.tensor_tensor(over, src[0:1, 0:E].unsqueeze(2).broadcast_to([1, E, NJ]), grid(K_J, E, NJ),
                                       ALU.is_gt))
                then(dve.tensor_reduce(n_slots, over, AX_X, ALU.add))
                sums = upto[:, 0:E * E].rearrange("p (a c) -> p a c", a=E)
                then(dve.tensor_tensor(sums, n_slots.unsqueeze(1).broadcast_to([1, E, E]), grid(K_LE, E, E), ALU.mult))
                then(dve.tensor_reduce(end, sums, AX_X, ALU.add))
                le_g = le[:, :].rearrange("p (a c) -> p a c", a=SLOTS)
                then(dve.tensor_tensor(le_g, end.unsqueeze(1).broadcast_to([1, SLOTS, E]), grid(K_S, SLOTS, E),
                                       ALU.is_le))
                then(dve.tensor_reduce(slot_f[:, 0, :], le_g, AX_X, ALU.add))
                then(dve.tensor_scalar(step, n_slots, -float(P), float(REG), ALU.mult, ALU.add))
                wle_g = wle[:, :].rearrange("p (a c) -> p a c", a=SLOTS)
                then(dve.tensor_tensor(wle_g, le_g, step.unsqueeze(1).broadcast_to([1, SLOTS, E]), ALU.mult))
                then(dve.tensor_reduce(slot_f[:, 1, :], wle_g, AX_X, ALU.add))
                then(dve.tensor_tensor(slot_g[:, :], slot_f[:, 1, :], one[:, K_S128:K_S128 + SLOTS], ALU.add))
                dve.tensor_scalar(slot_i[:, 0, :], slot_f[:, 0, :], float(E - 1), None, ALU.min)
                dve.tensor_scalar(slot_i[:, 1, :], slot_g[:, :], float(PAD_ROW), None, ALU.min).then_inc(slots_ready, 1)

            work = {"q": class_query, "k": keys, "cs": class_max, "ct": class_turned,
                    "pj": second_residual, "lg": choose, "rk": place_rows, "cn": fill_slots}

            dve.wait_ge(rout_w_in, 16 * 2)
            for kind, n in FIRST:
                work[kind](n, SPARE[kind, n])
            class_factors(0)
            for hh in range(len(PLAN)):
                if hh < HEADS:
                    maxes(hh)
                if hh < HEADS - 1 and hh % H == 7:
                    class_factors(hh // H + 1)
                if TURN_LAG <= hh < HEADS + TURN_LAG and hh % 2 == 0:
                    turned_probs(hh - TURN_LAG)
                if HG <= hh <= HEADS and hh % HG == 0:
                    ratios(hh // HG - 1)
                if hh >= VALUES_LAG and (hh - VALUES_LAG) % HG == 0:
                    finish_group((hh - VALUES_LAG) // HG)
                if hh < HEADS and hh % H == 3:
                    class_columns(hh // H)
                if H < hh < HEADS and hh % H == 5:
                    second_norm(hh // H - 1)
                for kind, n in PLAN[hh]:
                    if kind == "xr" and hh > HEADS:
                        second_norm(n)
                    if kind in work:
                        work[kind](n, SPARE[kind, n])

            def slot_norm(s):
                dve.wait_ge(xs_in, (s + 1) * 16)
                after_slots(dve, xt3_t, s)
                dve.tensor_scalar(xn3[:, :], xs[:, bass.ds(s * ROW, C)], xs[:, bass.ds(s * ROW + C, 1)],
                                  xs[:, bass.ds(s * ROW + C + 1, 1)], ALU.subtract, ALU.mult).then_inc(xn3_ready, 1)

            def slot_hidden(s):
                dve.wait_ge(gate_ready, s + 1)
                after_slots(dve, hid_t_t, s)
                dve.tensor_tensor(hid[:, :], gate[:, :], bank[1][:, :], ALU.mult).then_inc(hid_ready, 1)

            def slot_rows(s):
                dve.wait_ge(obf_ready, s + 1)
                after_slots(dve, y_out, s, 16)
                dve.tensor_copy(y_row[:, :], xs_i[:, bass.ds(s * ROW + C + 3, 1)])
                dve.scalar_tensor_tensor(out=y[:, :], in0=o_bf[:, :], scalar=xs[:, bass.ds(s * ROW + C + 2, 1)],
                                         in1=xs[:, bass.ds(s * ROW, C)], op0=ALU.mult, op1=ALU.add)\
                   .then_inc(y_ready, 1)

            slot_norm(0)
            slot_norm(1)
            slot_hidden(0)

            def slot_step(s):
                slot_norm(s + 1)
                slot_hidden(s)
                slot_rows(s - 1)

            slot_step(1)
            with dve.Fori(0, (SLOTS - 3) // STEPS) as turn:
                for step in range(STEPS):
                    slot_step(turn * STEPS + 2 + step)
            slot_hidden(SLOTS - 1)
            slot_rows(SLOTS - 2)
            slot_rows(SLOTS - 1)


def shape_constants():
    import numpy as np

    k = np.zeros((P, K_END), np.float32)
    p = np.arange(P)
    k[:, K_ID:K_ID + P] = np.eye(P)

    def interpolation(m):
        at = np.clip((np.arange(N) + 0.5) * (m / N) - 0.5, 0.0, m - 1)
        lo = np.floor(at).astype(int)
        w = np.zeros((m, N), np.float32)
        np.add.at(w, (lo, np.arange(N)), 1.0 - (at - lo))
        np.add.at(w, (np.minimum(lo + 1, m - 1), np.arange(N)), at - lo)
        return w

    w1, w2 = interpolation(N1), interpolation(N2)
    for odd in range(2):
        k[odd * N1:(odd + 1) * N1, K_I1 + odd * N:K_I1 + (odd + 1) * N] = w1
    for h in range(HG):
        k[h * D:(h + 1) * D, K_MQ + h] = 1.0
        for g in range(G):
            k[h * D:(h + 1) * D, K_M8 + g * H + g * HG + h] = 1.0
    for g in range(G):
        for h in range(HG):
            k[g * HG + h, K_SEL + g * P + h * HP:K_SEL + g * P + (h + 1) * HP] = 1.0
    k[:, K_E:K_E + E] = np.arange(E)
    k[:, K_BASE:K_BASE + E] = np.arange(E) * REG
    k[:, K_TRI:K_TRI + P] = p[:, None] < p[None, :]
    k[:, K_ONE:K_ONE + P] = 1.0
    k[0, K_J:K_J + E * NJ] = np.tile(np.arange(NJ) * P, E)
    k[0, K_LE:K_LE + E * E] = (np.arange(E)[None, :] <= np.arange(E)[:, None]).ravel()
    k[0, K_S:K_S + SLOTS * E] = np.repeat(np.arange(SLOTS), E)
    k[0, K_S128:K_S128 + SLOTS] = np.arange(SLOTS) * P
    two = np.zeros((P - L0, B, N), np.float32)
    for b in range(B):
        two[EMB - L0 + b * N2:EMB - L0 + (b + 1) * N2, b] = w2
    return k, two.reshape(P - L0, B * N)


def kernel(x, cls_tok, L0_tok_W0, L0_tok_b0, L0_tok_W1, L0_tok_b1, L0_tok_W2, L0_tok_b2, L0_tok_Wf, L0_tok_bf,
           L0_tok_idx0, L0_tok_idx1, L0_tok_idx2, L0_attn_w_qkv, L0_attn_w_proj, L0_attn_b_proj, L0_ffn_router_w,
           L0_ffn_router_b, L0_ffn_w1, L0_ffn_w2, L0_ffn_w3):
    import concourse.bacc as bacc
    import numpy as np
    from concourse.bass_utils import run_bass_kernel_spmd

    x = np.asarray(x)

    def patches(p):
        n = GRID // p
        t = x.reshape(B, CH, n, p, n, p).transpose(2, 4, 0, 3, 5, 1)
        return t.reshape(n * n, B * p * p * CH)

    idx0, idx1, idx2 = (np.asarray(a) for a in (L0_tok_idx0, L0_tok_idx1, L0_tok_idx2))
    idx = np.concatenate([
        idx2.reshape(N2, G2, GP // G2).transpose(1, 0, 2).reshape(P, GP // G2),
        idx1.reshape(N1, G1, GP // G1).transpose(1, 0, 2).reshape(P, GP // G1),
        idx0.reshape(HALVES, P, GP).transpose(1, 0, 2).reshape(P, HALVES * GP),
    ], axis=1)
    wproj = np.zeros((HG, HP, G, C), np.float32)
    wproj[:, 0:D] = np.asarray(L0_attn_w_proj).reshape(G, HG, D, C).transpose(1, 2, 0, 3)
    consts, interp2 = shape_constants()
    arrays = {
        "pix0": patches(1), "pix1": patches(2), "pix2": patches(4), "idx": idx,
        "lw": np.concatenate([np.asarray(a) for a in (L0_tok_W0, L0_tok_W1, L0_tok_W2)], axis=1),
        "wft": np.asarray(L0_tok_Wf).reshape(C, 3, EMB).transpose(2, 1, 0),
        "lb": np.stack([np.asarray(a) for a in (L0_tok_b0, L0_tok_b1, L0_tok_b2)], axis=1),
        "bf": np.asarray(L0_tok_bf).reshape(1, C), "cls_tok": np.asarray(cls_tok).reshape(1, C),
        "wqkv": L0_attn_w_qkv, "wproj": wproj.reshape(P, G, C),
        "bproj": np.asarray(L0_attn_b_proj).reshape(1, C), "rw": L0_ffn_router_w,
        "rb": np.asarray(L0_ffn_router_b).reshape(1, E), "w1": L0_ffn_w1, "w2": L0_ffn_w2, "w3": L0_ffn_w3,
        "consts": consts, "interp2": interp2,
    }
    arrays = {name: np.ascontiguousarray(a) for name, a in arrays.items()}
    nc = bacc.Bacc("TRN2", target_bir_lowering=False, num_devices=1)
    args = [nc.dram_tensor(name, a.shape, mybir.dt.from_np(a.dtype), kind="ExternalInput").ap()
            for name, a in arrays.items()]
    out = nc.dram_tensor("out", (B * S, C), F32, kind="ExternalOutput").ap()
    build(nc, *args, out)
    got = run_bass_kernel_spmd(nc, [arrays], core_ids=[0]).results[0]["out"]
    return got.reshape(B, S, C)
```

```python
from contextlib import ExitStack

import concourse.bass as bass
from concourse import mybir

ALU = mybir.AluOpType
ACT = mybir.ActivationFunctionType
AX_X = mybir.AxisListType.X
F32 = mybir.dt.float32
BF16 = mybir.dt.bfloat16
I32 = mybir.dt.int32
U32 = mybir.dt.uint32

B = 4
GRID = 64
CH = 3
GP = 16
N = GRID * GRID // GP
S = N + 1
C = 192
KH = C // 2
EMB = 64
H = 8
D = C // H
HG = 4
G = H // HG
HP = 32
GH = HG * D
P = 128
HALVES = N // P
TILES = B * HALVES + 1
CLS = TILES - 1
E = 8
HID = 512
HC = HID // P
ROW = C + 4
REG = (B * S + P - 1) // P * P
SLOTS = (B * S + E * (P - 1)) // P
MIN_SLOTS = (B * S + P - 1) // P
STEPS = 3
assert (MIN_SLOTS - 3) % STEPS == 0
PAD_ROW = E * REG
NO_ROW = 1 << 20
EPS = 1e-5
SCALE = float(D) ** -0.5

G1 = 2
G2 = 8
N1, N2 = N // 4, N // 16
V0, V1, V2 = CH, CH * 4, CH * 16
L0, L1, L2 = GP * V0, GP * V1, GP * V2
SELECTED = 14
RUN = GRID * GRID // P
GATHERS = GP // G2 + GP // G1 + HALVES * GP
COL1 = GP // G2
COL0 = COL1 + GP // G1

K_ID = 0
K_I1 = K_ID + P
K_MQ = K_I1 + 2 * HALVES * P
K_M8 = K_MQ + HG
K_SEL = K_M8 + G * H
K_E = K_SEL + G * P
K_BASE = K_E + E
K_TRI = K_BASE + E
K_ONE = K_TRI + P
K_J = K_ONE + P
NJ = REG // P
K_LE = K_J + E * NJ
K_S = K_LE + E * E
K_S128 = K_S + SLOTS * E
K_END = K_S128 + SLOTS


def build(nc, pix0, pix1, pix2, idx, idx_row, lw, wft, lb, bf, cls_tok, wqkv, wproj, bproj, rw, rb, w1, w2, w3,
          consts, interp2, out):
    with ExitStack() as ctx:
        def sb(name, shape, dt=F32):
            return ctx.enter_context(nc.sbuf_tensor(name, shape, dt))

        area = sb("area", [P, 2 * H * HALVES * S])

        def carve(at, *shape, of=area):
            n = 1
            for size in shape[1:]:
                n *= size
            names = " ".join("abcd"[:len(shape) - 1])
            sizes = dict(zip("abcd", shape[1:]))
            return of[0:shape[0], at:at + n].rearrange(f"p ({names}) -> p {names}", **sizes), at + n

        def sem(name):
            return ctx.enter_context(nc.semaphore(name))

        scratch = nc.dram_tensor("routed_rows", (PAD_ROW + P, ROW), F32, kind="Internal").ap()

        psum = ctx.enter_context(nc.psum_tensor("psum", [P, 8, 512], F32))
        bank = [psum[:, i, :] for i in range(8)]

        k = sb("k", [P, K_END])
        ident = k[:, K_ID:K_ID + P]
        idx_sb = sb("idx_sb", [P, GATHERS], I32)
        lw_sb, at = carve(0, EMB, L0 + L1 + L2)
        wft_sb, at = carve(at, EMB, 3, C)
        lb_sb = sb("lb_sb", [EMB, 3])
        lb_rep = sb("lb_rep", [EMB, 3, B * N2])
        bf_sb = sb("bf_sb", [1, C])
        wqkv_sb = sb("wqkv_sb", [KH, 2, 3 * C])
        wv_pad = sb("wv_pad", [KH, 2, H, HP])
        wproj_sb = sb("wproj_sb", [P, G, C])
        bproj_sb = sb("bproj_sb", [P, C])
        rw_sb = sb("rw_sb", [KH, 2, E])
        rb_sb = sb("rb_sb", [P, E])
        w12_sb = sb("w12_sb", [KH, E * 2 * 2 * HID])
        w3_sb = sb("w3_sb", [P, E * HC * C])
        tri_bf = sb("tri_bf", [P, P], BF16)
        one_bf = sb("one_bf", [P, P], BF16)

        which, end = carve(0, P, SELECTED, P, of=w3_sb)
        which = which.bitcast(I32)
        run_hot, end = carve(end, P, SELECTED, P, of=w3_sb)
        table, end = carve(end, P, RUN * B * V0, of=w3_sb)
        picked, end = carve(end, P, 2, RUN, B * V0, of=w3_sb)
        place_hot, end = carve(end, P, SELECTED, RUN, of=w3_sb)
        in_run, end = carve(end, P, SELECTED, of=w3_sb)
        counts, end = carve(end, P, RUN + 1, of=w3_sb)
        counts_f, end = carve(end, P, RUN + 1, of=w3_sb)

        px0, at = carve(at, P, HALVES * GP, B * V0)
        px1, at = carve(at, P, GP // G1, B * V1)
        px2, at = carve(at, P, GP // G2, B * V2)
        px0b, end = carve(end, P, HALVES, B, GP * V0, of=w3_sb)
        px1b, at = carve(at, P, B, L1 // G1)
        px2b, at = carve(at, P, B, L2 // G2)
        px1t, at = carve(at, L1 // G1, G1, B, N1)
        px2t, at = carve(at, L2 // G2, G2, B, N2)
        c1, at = carve(at, L1 // G1, G1, C)
        c2, at = carve(at, L2 // G2, G2, C)
        tok_l, at = carve(at, P, B, HALVES, P)
        tok_r = sb("tok_r", [P, C])
        f1, at = carve(at, P, 2, C)
        cls_x = sb("cls_x", [B, C])
        stat1 = sb("stat1", [P, TILES, 6])
        mv1 = sb("mv1", [P, TILES, 2])
        half_neg = sb("half_neg", [P, TILES])
        rstd1 = sb("rstd1", [P, TILES])
        xn1 = sb("xn1", [P, B, C])
        xn1c = sb("xn1c", [B, C])
        xt1 = sb("xt1", [KH, 2, B, S])

        v_sb = sb("v_sb", [P, B, HALVES, H, HP])
        vcls = sb("vcls", [P, G, B])
        q_sb = sb("q_sb", [GH, S])
        q_head = sb("q_head", [GH, 2, G, HG, N])
        q_cls = sb("q_cls", [GH, 2, G, H])
        k_sb = sb("k_sb", [GH, 2, G, S])
        nmax = sb("nmax", [P, H, HALVES])
        den = sb("den", [P, H, HALVES])
        rp = sb("rp", [P, 2, HALVES, H])
        rp_rows = sb("rp_rows", [P, 2, HALVES, HG * HP])
        probs, at = carve(0, P, H, HALVES, S)
        pt, at = carve(at, P, H, HALVES, S)
        nmax_c = sb("nmax_c", [H, 1])
        rp_c = sb("rp_c", [H, 2])
        den_c = sb("den_c", [H, 1])
        col = sb("col", [P, HALVES, H])
        probs_c = sb("probs_c", [H, S])
        rpt = sb("rpt", [P, 2, S])
        part = sb("part", [P, S])
        ot = sb("ot", [P, B, G, S])
        rpc = sb("rpc", [P, 2, G, 2])

        rows = sb("rows", [P, TILES, ROW])
        h1 = rows[:, :, 0:C]
        rows_i = rows[:, :, :].bitcast(I32)
        stat2 = sb("stat2", [P, 2, 6])
        vare = sb("vare", [P, TILES])
        xn2 = sb("xn2", [P, 2, C])
        xt2 = sb("xt2", [KH, 2, 2, P])
        logits = sb("logits", [P, 2, E])
        top = sb("top", [P, 2, E])
        topi = sb("topi", [P, 2, E], U32)
        ntop = sb("ntop", [P, 2])
        prob_e = sb("prob_e", [P, 2, E])
        prob_s = sb("prob_s", [P, 2])
        chosen = sb("chosen", [P, TILES, E], BF16)
        place = sb("place", [P, 2, E])
        place2 = sb("place2", [P, 2, E])
        pos = sb("pos", [P, TILES])
        pos_i = sb("pos_i", [P, TILES], I32)
        empty = sb("empty", [P, 1, ROW])
        slot_f = sb("slot_f", [1, 2, SLOTS])
        slot_g = sb("slot_g", [1, SLOTS])
        slot_i = sb("slot_i", [1, 3, SLOTS], I32)

        xs, at = carve(0, P, SLOTS * ROW)
        xs_i = xs[:, :].bitcast(I32)
        xn3, at = carve(at, P, C)
        xt3, at = carve(at, KH, 2, P)
        gate, at = carve(at, P, HID)
        hid, at = carve(at, P, HID)
        hid_t, at = carve(at, P, HC, P)
        o_bf = sb("o_bf", [P, C], BF16)
        y, at = carve(at, P, C)
        y_row = sb("y_row", [P, 1], U32)

        nt, at = carve(at, 1, E * NJ + 6 * E)
        upto, at = carve(at, 1, E * E + E)
        le, at = carve(at, 1, SLOTS * E)
        wle, at = carve(at, 1, SLOTS * E)
        idx_in, lw_in, wft_in, k_in, int2_in, small_in, wqkv_in, attn_w_in, rout_w_in = (
            sem(n) for n in ("idx_in", "lw_in", "wft_in", "k_in", "int2_in", "small_in", "wqkv_in", "attn_w_in",
                             "rout_w_in"))
        w_in = [sem(f"w{e}_in") for e in range(E)]
        px2_in, px1_in = sem("px2_in"), sem("px1_in")
        px0_in = [sem(f"px0_in{i}") for i in range(HALVES)]
        px0_ev_act = sem("px0_ev_act")
        px2_by_image, px1_by_image, px0_by_image = sem("px2_by_image"), sem("px1_by_image"), sem("px0_by_image")
        which_in, table_in, counts_ready, place_hot_ready = (
            sem(n) for n in ("which_in", "table_in", "counts_ready", "place_hot_ready"))
        run_ready, run_hot_ready, pick_mm, picked_ready, pick_done = (
            sem(n) for n in ("run_ready", "run_hot_ready", "pick_mm", "picked_ready", "pick_done"))
        prep = sem("prep")
        consts_bf, lb_ready = sem("consts_bf"), sem("lb_ready")
        cw_mm, cw_ev = sem("cw_mm"), sem("cw_ev")
        clsn, cls_t, cls_ev, vcls_mm, vcls_ev = (sem(n) for n in ("clsn", "cls_t", "cls_ev", "vcls_mm", "vcls_ev"))
        px2_t, px2_ev, f2_mm, f2_ev = (sem(n) for n in ("px2_t", "px2_ev", "f2_mm", "f2_ev"))
        px1_t, px1_ev, f1_mm, f1_ev = (sem(n) for n in ("px1_t", "px1_ev", "f1_mm", "f1_ev"))
        px0_t, px0_ev = sem("px0_t"), sem("px0_ev")
        tok_mm, var1_ready, rstd1_ready, xn1_ready = (
            sem(n) for n in ("tok_mm", "var1_ready", "rstd1_ready", "xn1_ready"))
        xt1_t, xt1_ev, v_mm, v_ev = (sem(n) for n in ("xt1_t", "xt1_ev", "v_mm", "v_ev"))
        q_mm, q_in, k_mm, q_ev, k_ev, qc_ev = (sem(n) for n in ("q_mm", "q_in", "k_mm", "q_ev", "k_ev", "qc_ev"))
        sc_mm, max_ready, exp_ready, p_t, pt_dve, pt_act, pv_mm = (
            sem(n) for n in ("sc_mm", "max_ready", "exp_ready", "p_t", "pt_dve", "pt_act", "pv_mm"))
        csc_mm, cmax_ready, cexp_ready, crp_ready, cp_t, cp_ev = (
            sem(n) for n in ("csc_mm", "cmax_ready", "cexp_ready", "crp_ready", "cp_t", "cp_ev"))
        rp_rows_ready, col_ready = sem("rp_rows_ready"), sem("col_ready")
        rp_ready, rp_t, rp_ev, rpc_ready, part_ready, ot_ready = (
            sem(n) for n in ("rp_ready", "rp_t", "rp_ev", "rpc_ready", "part_ready", "ot_ready"))
        proj_mm, h2_ready, var2_ready, rstd2_ready, xn2_ready, xt2_t, xt2_ev = (
            sem(n) for n in ("proj_mm", "h2_ready", "var2_ready", "rstd2_ready", "xn2_ready", "xt2_t", "xt2_ev"))
        lg_mm, lg_ready, ntop_ready, pexp_ready, prob_ready, chosen_ready, rank_mm, place_ready, pos_ready = (
            sem(n) for n in ("lg_mm", "lg_ready", "ntop_ready", "pexp_ready", "prob_ready", "chosen_ready", "rank_mm",
                             "place_ready", "pos_ready"))
        row_ids, empty_ready, empty_out, row_out, cnt_mm, slots_ready = (
            sem(n) for n in ("row_ids", "empty_ready", "empty_out", "row_out", "cnt_mm", "slots_ready"))
        xs_in, xn3_ready, xt3_t, xt3_ev, up_mm, gate_ready, hid_ready, hid_t_t, hid_t_ev, down_mm, obf_ready, y_ready = (
            sem(n) for n in ("xs_in", "xn3_ready", "xt3_t", "xt3_ev", "up_mm", "gate_ready", "hid_ready", "hid_t_t",
                             "hid_t_ev", "down_mm", "obf_ready", "y_ready"))
        y_out, dve_done, h1_ready = (sem(n) for n in ("y_out", "dve_done", "h1_ready"))

        block = ctx.enter_context(nc.Block())

        MISC = (6, 7)
        HEADS = B * H
        PLAN = []
        for b in range(B):
            prev, nxt = b > 0, b + 1 < B
            PLAN += [
                [("ct", b)] + [("rk", b - 2)] * (b > 1),
                [("f", G * b - 1)] * prev + [("q", G * (b + 1))] * nxt,
                [("k", G * (b + 1))] * nxt,
                [("pj", b - 1)] * prev,
                [("q", G * (b + 1) + 1)] * nxt,
                [("f", G * b)] + [("k", G * (b + 1) + 1)] * nxt,
                [("cs", b + 1)] * nxt + [("xr", b - 1)] * prev,
                [("lg", b - 1)] * prev,
            ]
        PLAN += [[("rk", B - 2)], [("f", G * B - 1)], [],
                 [("pj", B - 1), ("pj", B), ("xr", B - 1), ("lg", B - 1), ("xr", B), ("rk", B - 1), ("lg", B),
                  ("rk", B), ("cn", 0)]]
        PLAN[0] = []
        PLAN[1], PLAN[2], PLAN[3] = [("q", 1)], [("k", 1)] + PLAN[1], PLAN[2] + [("cs", 0)]
        PLAN[5] = [("ct", 0)] + PLAN[5]
        TURN_LAG = 2
        VALUES_LAG = 6

        FIRST = [("q", 0), ("k", 0)]
        SPARE = {task: bank[MISC[i % 2]] for i, task in enumerate(FIRST + sum(PLAN, []))}

        def after_slots(eng, signal, s, each=1):
            if not (isinstance(s, int) and s == 0):
                eng.wait_ge(signal, s * each)

        def used_slots(eng):
            eng.wait_ge(slots_ready, 1)
            return eng.value_load(slot_i[0:1, 2, 0:1], min_val=MIN_SLOTS, max_val=SLOTS)

        def while_used(eng, used, s, step, finish, state=None):
            if s == SLOTS:
                finish(s - 1, state)
                return
            with eng.If(used == s):
                finish(s - 1, state)
            with eng.If(used > s):
                while_used(eng, used, s + 1, step, finish, step(s, state))

        @block.sync
        def _(sp):
            sp.dma_start(idx_sb[:, :], idx).then_inc(idx_in, 16)
            sp.dma_start(which, idx_row.broadcast_to([P, SELECTED * P]).rearrange("p (g n) -> p g n", n=P))\
              .then_inc(which_in, 16)
            sp.dma_start(table, pix0.rearrange("(p t) c -> p (t c)", p=P)).then_inc(table_in, 16)
            sp.dma_start(lw_sb[:, :], lw).then_inc(lw_in, 16)
            sp.dma_start(wft_sb[:, :, :], wft).then_inc(wft_in, 16)
            sp.dma_start(tok_l[L0:P, :, :, :].rearrange("p b h n -> p (b h n)"), interp2).then_inc(int2_in, 16)
            sp.dma_start(wqkv_sb[:, :, :], wqkv.rearrange("(p t) n -> p t n", t=2)).then_inc(wqkv_in, 16)
            sp.dma_start(wproj_sb[:, :, :], wproj).then_inc(attn_w_in, 16)
            sp.dma_start(rw_sb[:, :, :], rw.rearrange("(p t) n -> p t n", t=2)).then_inc(rout_w_in, 16)
            sp.dma_start(rb_sb[:, :], rb.broadcast_to([P, E])).then_inc(rout_w_in, 16)
            sp.wait_ge(empty_ready, 1)
            sp.wait_ge(px0_ev_act, 1)
            for e in range(E):
                sp.dma_start(scratch[e * REG:(e + 1) * REG, :].rearrange("(p t) c -> p t c", p=P),
                             empty[:, :, :].broadcast_to([P, REG // P, ROW])).then_inc(empty_out, 16)
            sp.dma_start(scratch[PAD_ROW:PAD_ROW + P, :], empty[:, 0, :]).then_inc(empty_out, 16)
            for e in range(E):
                for i, w in enumerate((w1, w2)):
                    at = (2 * e + i) * 2 * HID
                    sp.dma_start(w12_sb[:, at:at + 2 * HID],
                                 w[e].rearrange("(p t) n -> p (t n)", t=2)).then_inc(w_in[e], 16)
                sp.dma_start(w3_sb[:, e * HC * C:(e + 1) * HC * C],
                             w3[e].rearrange("(p t) n -> p (t n)", t=HC)).then_inc(w_in[e], 16)
            sp.wait_ge(slots_ready, 1)
            sp.wait_ge(row_out, 16 * TILES)
            def load_slot(s):
                first = sp.value_load(slot_i[0:1, 1, bass.ds(s, 1)], min_val=0, max_val=PAD_ROW)
                after_slots(sp, xs_in, s, 16)
                sp.dma_start(xs[:, bass.ds(s * ROW, ROW)], scratch[bass.ds(first, P), :]).then_inc(xs_in, 16)

            load_slot(0)
            with sp.Fori(1, SLOTS) as s:
                load_slot(s)
            sp.wait_ge(xs_in, 16 * SLOTS)

        def tiles(b):
            return (HALVES * b, HALVES, P) if b < B else (CLS, 1, B)

        @block.gpsimd
        def _(pool):
            def gather(dst, src, col, signal):
                pool.indirect_dma_start(
                    out=dst, out_offset=None, in_=src,
                    in_offset=bass.IndirectOffsetOnAxis(ap=idx_sb[:, col:col + 1].bitcast(U32), axis=0),
                ).then_inc(signal, 16)

            def inverse_deviation(dst, var, n, signal):
                pool.tensor_tensor(dst, var, half_neg[:, 0:n][0:dst.shape[0]], ALU.pow).then_inc(signal, 1)

            pool.iota(counts[:, 0:RUN].bitcast(I32), [[1, RUN]], base=0, channel_multiplier=0).then_inc(counts_ready, 1)
            pool.iota(counts[:, RUN:RUN + 1].bitcast(I32), [[0, 1]], base=0, channel_multiplier=1)\
                .then_inc(counts_ready, 1)
            pool.wait_ge(idx_in, 16)
            for g in range(GP // G2):
                gather(px2[:, g, :], pix2, g, px2_in)
            for g in range(GP // G1):
                gather(px1[:, g, :], pix1, COL1 + g, px1_in)
            pool.wait_ge(prep, 2)
            pool.wait_ge(var1_ready, 1)
            inverse_deviation(rstd1[0:B, CLS:TILES], mv1[0:B, CLS, 1:2], 1, rstd1_ready)
            for g in range(GP):
                gather(px0[:, g, :], pix0, COL0 + g, px0_in[0])
            for g in range(GP - SELECTED):
                gather(px0[:, GP + g, :], pix0, COL0 + GP + g, px0_in[1])
            pool.iota(rows_i[:, 0:CLS, C + 3], [[S, B], [P, HALVES]], base=1,
                      channel_multiplier=1).then_inc(row_ids, 1)
            pool.iota(rows_i[0:B, CLS, C + 3:C + 4], [[0, 1]], base=0, channel_multiplier=S).then_inc(row_ids, 1)
            for pair in range(2):
                pool.wait_ge(var1_ready, 2 + pair)
                inverse_deviation(rstd1[:, B * pair:B * (pair + 1)], mv1[:, B * pair:B * (pair + 1), 1], B, rstd1_ready)

            def scatter(t, n):
                pool.indirect_dma_start(
                    out=scratch, out_offset=bass.IndirectOffsetOnAxis(ap=pos_i[0:n, t:t + 1].bitcast(U32), axis=0),
                    in_=rows[0:n, t, :], in_offset=None).then_inc(row_out, 16)

            def row_deviations(b):
                pool.wait_ge(var2_ready, b + 1)
                t, n, m = tiles(b)
                inverse_deviation(rows[0:m, t:t + n, C + 1], vare[0:m, t:t + n], n, rstd2_ready)

            def send_rows(b):
                t, n, m = tiles(b)
                pool.wait_ge(pos_ready, b + 1)
                pool.wait_ge(rstd2_ready, b + 1)
                pool.wait_ge(row_ids, 2)
                if b == 0:
                    pool.wait_ge(empty_out, 16 * (E + 1))
                for i in range(n):
                    scatter(t + i, m)

            def spread_queries(n):
                b, g = divmod(n, G)
                pool.wait_ge(q_in, n + 1)
                if b >= 2:
                    pool.wait_ge(sc_mm, H * (b - 1))
                for h in range(HG):
                    pool.tensor_scalar(q_head[:, b % 2, g, h, :], q_sb[:, 0:N], k[0:GH, K_MQ + h:K_MQ + h + 1], None,
                                       ALU.mult).then_inc(q_ev, 1)

            work = {"q": spread_queries, "pj": row_deviations, "rk": send_rows}
            for kind, n in FIRST + sum(PLAN, []):
                if kind in work:
                    work[kind](n)

            def slot_out(s, _=None):
                pool.wait_ge(y_ready, s + 1)
                pool.indirect_dma_start(out=out, out_offset=bass.IndirectOffsetOnAxis(ap=y_row[:, 0:1], axis=0),
                                        in_=y[:, :], in_offset=None, bounds_check=B * S - 1,
                                        oob_is_err=False).then_inc(y_out, 16)

            used = used_slots(pool)
            for s in range(MIN_SLOTS):
                slot_out(s)
            while_used(pool, used, MIN_SLOTS, slot_out, lambda s, _: pool.wait_ge(y_out, 16 * (s + 1)))

        def probs_in(eng, hh):
            eng.wait_ge(pt_dve, (hh + 2) // 2)
            if hh >= 1:
                eng.wait_ge(pt_act, (hh + 1) // 2)

        @block.tensor
        def _(pe):
            def mm(dst, lhs, rhs, first, last):
                return pe.matmul(dst, lhs, rhs, start=first, stop=last)

            def keep_warm(n, dst):
                for _ in range(n):
                    mm(dst, ident, k[:, 0:512], True, True)

            def pick_runs(j):
                pe.wait_ge(run_hot_ready, j + 1)
                if j >= 2:
                    pe.wait_ge(picked_ready, j - 1)
                for i in range(2):
                    last = mm(bank[2 * (j % 2) + i][:, 0:RUN * B * V0], run_hot[:, 2 * j + i, :], table, True, True)
                last.then_inc(pick_mm, 1)

            pe.wait_ge(table_in, 16)
            for j in range(2):
                pick_runs(j)

            pe.wait_ge(lw_in, 16)
            pe.wait_ge(wft_in, 16)
            rounds = [[(0, L0, 0)], [(L0 + (L1 // G1) * g, L1 // G1, 1) for g in range(G1)]]
            rounds += [[(L0 + L1 + (L2 // G2) * g, L2 // G2, 2) for g in (j, j + 1)] for j in range(0, G2, 2)]
            for r, work in enumerate(rounds):
                if r == 2:
                    pick_runs(2)
                if r >= 2:
                    pe.wait_ge(cw_ev, r - 1)
                for i, (at, m, level) in enumerate(work):
                    last = mm(bank[MISC[r % 2]][0:m, i * C:(i + 1) * C], lw_sb[:, at:at + m], wft_sb[:, level, :],
                              True, True)
                last.then_inc(cw_mm, 1)

            pick_runs(3)
            pe.wait_ge(k_in, 16)
            pe.wait_ge(px2_by_image, 1)
            for b in range(B):
                last = pe.transpose(bank[5][0:L2 // G2, b * P:(b + 1) * P], px2b[:, b, :], ident)
            last.then_inc(px2_t, 1)

            pick_runs(4)
            pe.wait_ge(px2_ev, 1)
            pe.wait_ge(cw_ev, len(rounds))
            pe.wait_ge(lb_ready, 1)
            pe.wait_ge(small_in, 16 * 3)
            f2_ps = bank[4][EMB:P, 0:C]
            for g in range(G2):
                mm(f2_ps, px2t[:, g, :, :].rearrange("p b m -> p (b m)"), c2[:, g, :], g == 0, False)
            for level in range(3):
                mm(f2_ps, lb_rep[:, level, :], wft_sb[:, level, :], False, False)
            mm(f2_ps, k[0:1, K_ONE:K_ONE + B * N2], bf_sb[:, :], False, True).then_inc(f2_mm, 1)
            pe.wait_ge(px1_by_image, 1)
            for b in range(B):
                last = pe.transpose(bank[5][0:L1 // G1, b * P:(b + 1) * P], px1b[:, b, :], ident)
            last.then_inc(px1_t, 1)

            pick_runs(5)
            pe.wait_ge(px1_ev, 1)
            pe.wait_ge(f2_ev, 1)
            for pair in range(2):
                for g in range(G1):
                    last = mm(bank[4][:, pair * C:(pair + 1) * C],
                              px1t[:, g, 2 * pair:2 * pair + 2, :].rearrange("p b m -> p (b m)"), c1[:, g, :],
                              g == 0, g == G1 - 1)
            last.then_inc(f1_mm, 1)
            pe.wait_ge(clsn, 1)
            for t in range(2):
                last = pe.transpose(bank[5][0:KH, t * B:(t + 1) * B], xn1c[:, t:C:2], ident[0:B, 0:B])
            last.then_inc(cls_t, 1)

            pick_runs(6)
            pe.wait_ge(cls_ev, 1)
            pe.wait_ge(f1_ev, 1)
            pe.wait_ge(prep, 5)
            for g in range(G):
                for t in range(2):
                    last = mm(bank[4][:, g * B:(g + 1) * B],
                              wv_pad[:, t, g * HG:(g + 1) * HG, :].rearrange("p h d -> p (h d)"),
                              xt1[:, t, :, N], t == 0, t == 1)
            last.then_inc(vcls_mm, 1)

            for half in range(HALVES):
                keep_warm(2, bank[7][:, :])
                pe.wait_ge(px0_by_image, half + 1)
                if half == 0:
                    pe.wait_ge(vcls_ev, 1)
                for b in range(B):
                    last = pe.transpose(bank[5 - half][0:L0, b * P:(b + 1) * P], px0b[:, half, b, :], ident)
                last.then_inc(px0_t, 1)

            pe.wait_ge(px0_ev, 1)
            pe.wait_ge(px0_ev_act, 1)
            pe.wait_ge(int2_in, 16)
            pe.wait_ge(f1_ev, 1)
            pe.wait_ge(picked_ready, SELECTED // 2)
            for b in range(B):
                for half in range(HALVES):
                    dst = bank[b][:, half * C:(half + 1) * C]
                    mm(dst, tok_l[:, b, half, :], tok_r[:, :], True, False)
                    at = K_I1 + ((b % 2) * HALVES + half) * P
                    last = mm(dst, k[:, at:at + P], f1[:, b // 2, :], False, True)
                last.then_inc(tok_mm, 1)

            keep_warm(1, bank[7][:, :])
            for n in range(CLS + 1):
                b, half = divmod(n, HALVES)
                if n < CLS:
                    pe.wait_ge(xn1_ready, n + 1)
                    if n >= 2:
                        pe.wait_ge(xt1_ev, n - 1)
                    for t in range(2):
                        last = pe.transpose(bank[MISC[n % 2]][0:KH, t * P:(t + 1) * P], xn1[:, n % B, t:C:2], ident)
                    last.then_inc(xt1_t, 1)
                if n == 0:
                    continue
                n -= 1
                b, half = divmod(n, HALVES)
                pe.wait_ge(xt1_ev, n + 1)
                if n >= 2:
                    pe.wait_ge(v_ev, n - 1)
                for t in range(2):
                    last = mm(bank[4 + n % 2][:, 0:C], xt1[:, t, b, half * P:(half + 1) * P],
                              wqkv_sb[:, t, 2 * C:3 * C], t == 0, t == 1)
                last.then_inc(v_mm, 1)

            def queries_or_keys(kind, n, dst):
                b, g = divmod(n, G)
                at = (0 if kind == "q" else C) + g * GH
                for t in range(2):
                    last = mm(dst[0:GH, 0:S], wqkv_sb[:, t, at:at + GH], xt1[:, t, b, :], t == 0, t == 1)
                last.then_inc(q_mm if kind == "q" else k_mm, 1)

            def class_scores(b, dst):
                pe.wait_ge(qc_ev, G * (b + 1))
                pe.wait_ge(k_ev, G * (b + 1))
                for g in range(G):
                    last = mm(dst[0:H, 0:S], q_cls[:, b % 2, g, :], k_sb[:, b % 2, g, :], g == 0, g == G - 1)
                last.then_inc(csc_mm, 1)

            def class_turn(b, dst):
                pe.wait_ge(crp_ready, b + 1)
                for i in range(HALVES):
                    pe.transpose(dst[:, i * H:(i + 1) * H], probs_c[:, i * P:(i + 1) * P], ident[0:H, 0:H])
                for g in range(G):
                    last = mm(dst[:, 32 + 2 * g:34 + 2 * g], k[0:H, K_SEL + g * P:K_SEL + (g + 1) * P], rp_c[:, :],
                              True, True)
                last.then_inc(cp_t, 1)

            def scores(hh):
                b, h = divmod(hh, H)
                pe.wait_ge(q_ev, hh + 1)
                if h % HG == 0:
                    pe.wait_ge(k_ev, hh // HG + 1)
                if hh >= 2:
                    pe.wait_ge(exp_ready, 2 * (hh - 1))
                for i in range(HALVES):
                    last = mm(bank[2 * (hh % 2) + i][:, 0:S], q_head[:, b % 2, h // HG, h % HG, i * P:(i + 1) * P],
                              k_sb[:, b % 2, h // HG, :], True, True)
                last.then_inc(sc_mm, 1)

            def turn_probs(hh):
                h = hh % H
                pe.wait_ge(exp_ready, 2 * (hh + 1))
                if hh:
                    probs_in(pe, hh - 1)
                for i in range(HALVES):
                    for j in range(HALVES):
                        last = pe.transpose(bank[5][:, (j * HALVES + i) * P:(j * HALVES + i + 1) * P],
                                            probs[:, h, i, j * P:(j + 1) * P], ident)
                last.then_inc(p_t, 1)

            def values(n):
                b, g = divmod(n, G)
                probs_in(pe, HG * (n + 1) - 1)
                if g == 0:
                    pe.wait_ge(col_ready, b + 1)
                if n:
                    pe.wait_ge(part_ready, n)
                for j in range(HALVES):
                    for q in range(HG):
                        h = g * HG + q
                        last = mm(bank[4][q * HP:(q + 1) * HP, 0:S], v_sb[:, b, j, h, :], pt[:, h, j, :],
                                  j == 0, j == HALVES - 1)
                last.then_inc(pv_mm, 1)

            def factors(n, dst):
                pe.wait_ge(rp_rows_ready, n + 1)
                for w in range(2):
                    for i in range(HALVES):
                        at = (w * HALVES + i) * P
                        last = pe.transpose(dst[:, at:at + P], rp_rows[:, w, i, :], ident)
                last.then_inc(rp_t, 1)

            def project(b, dst):
                if b < B:
                    pe.wait_ge(ot_ready, G * (b + 1))
                n = HALVES if b < B else 1
                for i in range(n):
                    for g in range(G):
                        lhs, m = (ot[:, b, g, i * P:(i + 1) * P], P) if b < B else (ot[:, :, g, N], B)
                        last = mm(dst[0:m, i * C:(i + 1) * C], lhs, wproj_sb[:, g, :], g == 0, g == G - 1)
                last.then_inc(proj_mm, 1)

            def turn_rows(b, dst):
                _, n, m = tiles(b)
                pe.wait_ge(xn2_ready, b + 1)
                for i in range(n):
                    for t in range(2):
                        last = pe.transpose(dst[0:KH, (i * 2 + t) * P:(i * 2 + t) * P + m], xn2[0:m, i, t:C:2],
                                            ident[0:m, 0:m])
                last.then_inc(xt2_t, 1)

            def route(b, dst):
                _, n, m = tiles(b)
                pe.wait_ge(xt2_ev, b + 1)
                for i in range(n):
                    for t in range(2):
                        last = mm(dst[0:m, i * E:(i + 1) * E], xt2[:, i, t, 0:m], rw_sb[:, t, :], t == 0, t == 1)
                last.then_inc(lg_mm, 1)

            def rank(b, dst):
                t0, n, m = tiles(b)
                pe.wait_ge(chosen_ready, b + 1)
                for i in range(n):
                    for before in range(t0 + i):
                        mm(dst[0:m, i * E:(i + 1) * E], one_bf[:, 0:m], chosen[:, before, :], before == 0, False)
                    last = mm(dst[0:m, i * E:(i + 1) * E], tri_bf[0:m, 0:m], chosen[0:m, t0 + i, :], t0 + i == 0, True)
                last.then_inc(rank_mm, 1)

            def count(_, dst):
                for t in range(TILES):
                    m = P if t < CLS else B
                    last = mm(dst[0:1, 0:E], one_bf[0:m, 0:1], chosen[0:m, t, :], t == 0, t == TILES - 1)
                last.then_inc(cnt_mm, 1)

            work = {
                "q": (lambda n, dst: queries_or_keys("q", n, dst), q_in), "k": (lambda n, dst: queries_or_keys("k", n, dst), k_ev),
                "cs": (class_scores, cexp_ready), "ct": (class_turn, cp_ev), "f": (factors, rp_ev),
                "pj": (project, h2_ready), "xr": (turn_rows, xt2_ev), "lg": (route, lg_ready), "rk": (rank, place_ready),
                "cn": (count, slots_ready),
            }
            last_turns = []

            def spare(kind, n):
                if len(last_turns) >= 2:
                    before, m = last_turns[-2]
                    pe.wait_ge(work[before][1], m + 1)
                last_turns.append((kind, n))
                work[kind][0](n, SPARE[kind, n])

            pe.wait_ge(rout_w_in, 16 * 2)
            pe.wait_ge(attn_w_in, 16 * 2)
            pe.wait_ge(consts_bf, 2)
            pe.wait_ge(v_ev, CLS)
            pe.wait_ge(h1_ready, TILES)
            for task in FIRST:
                spare(*task)
            for hh in range(len(PLAN)):
                if hh < HEADS:
                    scores(hh)
                if TURN_LAG <= hh < HEADS + TURN_LAG:
                    turn_probs(hh - TURN_LAG)
                if hh >= VALUES_LAG and (hh - VALUES_LAG) % HG == 0:
                    values((hh - VALUES_LAG) // HG)
                for task in PLAN[hh]:
                    spare(*task)

            keep_warm(7, bank[5][:, :])

            def slot_turn(s):
                pe.wait_ge(xn3_ready, s + 1)
                for t in range(2):
                    last = pe.transpose(bank[2][0:KH, t * P:(t + 1) * P], xn3[:, t:C:2], ident)
                last.then_inc(xt3_t, 1)

            def expert_of(s):
                return pe.value_load(slot_i[0:1, 0, bass.ds(s, 1)], min_val=0, max_val=E - 1)

            def slot_up(s, e):
                pe.wait_ge(xt3_ev, s + 1)
                for i in range(2):
                    for t in range(2):
                        last = mm(bank[i][:, :], xt3[:, t, :],
                                  w12_sb[:, bass.ds(e * (4 * HID) + (i * 2 + t) * HID, HID)], t == 0, t == 1)
                last.then_inc(up_mm, 1)

            def slot_down(s, e):
                pe.wait_ge(hid_t_ev, s + 1)
                after_slots(pe, obf_ready, s)
                for c in range(HC):
                    last = mm(bank[4][:, 0:C], hid_t[:, c, :], w3_sb[:, bass.ds(e * (HC * C) + c * C, C)],
                              c == 0, c == HC - 1)
                last.then_inc(down_mm, 1)

            def slot_turn_hidden(s):
                pe.wait_ge(hid_ready, s + 1)
                for c in range(HC):
                    last = pe.transpose(bank[3][:, c * P:(c + 1) * P], hid[:, c:HID:HC], ident)
                last.then_inc(hid_t_t, 1)

            used = used_slots(pe)
            for e in range(E):
                pe.wait_ge(w_in[e], 16 * 3)
            def slot_step(s, experts):
                before, e = experts
                slot_up(s, e)
                if not isinstance(s, int) or s + 1 < SLOTS:
                    slot_turn(s + 1)
                slot_down(s - 1, before)
                following = e, (expert_of(s + 1) if not isinstance(s, int) or s + 1 < SLOTS else e)
                slot_turn_hidden(s)
                return following

            slot_turn(0)
            experts = expert_of(0), expert_of(1)
            slot_up(0, experts[0])
            slot_turn(1)
            slot_turn_hidden(0)
            experts = slot_step(1, experts)
            slot_step(2, experts)
            with pe.Fori(0, (MIN_SLOTS - 3) // STEPS) as turn:
                experts = expert_of(turn * STEPS + 2), expert_of(turn * STEPS + 3)
                for step in range(STEPS):
                    experts = slot_step(turn * STEPS + 3 + step, experts)
            experts = expert_of(MIN_SLOTS - 1), expert_of(MIN_SLOTS)
            while_used(pe, used, MIN_SLOTS, slot_step, lambda s, experts: slot_down(s, experts[0]), experts)

        @block.scalar
        def _(act):
            act.dma_start(k[:, :], consts).then_inc(k_in, 16)
            act.dma_start(cls_x[:, :], cls_tok.broadcast_to([B, C])).then_inc(small_in, 16)
            act.dma_start(bf_sb[:, :], bf).then_inc(small_in, 16)
            act.dma_start(lb_sb[:, :], lb).then_inc(small_in, 16)
            act.dma_start(bproj_sb[:, :], bproj.broadcast_to([P, C])).then_inc(attn_w_in, 16)

            def copy(dst, src):
                return act.activation(dst, src, ACT.Copy)

            act.wait_ge(prep, 1)
            act.wait_ge(cw_mm, 1)
            copy(tok_r[0:L0, :], bank[MISC[0]][0:L0, 0:C]).then_inc(cw_ev, 1)
            act.wait_ge(cw_mm, 2)
            copy(c1[:, :, :], bank[MISC[1]][0:L1 // G1, 0:2 * C].rearrange("p (g c) -> p g c", g=2)).then_inc(cw_ev, 1)
            for j in range(G2 // 2):
                act.wait_ge(cw_mm, 3 + j)
                copy(c2[:, 2 * j:2 * j + 2, :],
                     bank[MISC[j % 2]][0:L2 // G2, 0:2 * C].rearrange("p (g c) -> p g c", g=2)).then_inc(cw_ev, 1)
            act.wait_ge(f2_mm, 1)
            copy(tok_r[EMB:P, :], bank[4][EMB:P, 0:C]).then_inc(f2_ev, 1)
            act.wait_ge(f1_mm, 1)
            copy(f1[:, :, :], bank[4][:, 0:2 * C].rearrange("p (g c) -> p g c", g=2)).then_inc(f1_ev, 1)

            act.wait_ge(prep, 4)
            def rows_turned(n):
                b, half = divmod(n, HALVES)
                act.wait_ge(xt1_t, n + 1)
                copy(xt1[:, :, b, half * P:(half + 1) * P],
                     bank[MISC[n % 2]][0:KH, 0:2 * P].rearrange("p (t n) -> p t n", t=2)).then_inc(xt1_ev, 1)

            def values_made(n):
                b, half = divmod(n, HALVES)
                act.wait_ge(v_mm, n + 1)
                copy(v_sb[:, b, half, :, 0:D],
                     bank[4 + n % 2][:, 0:C].rearrange("p (h d) -> p h d", h=H)).then_inc(v_ev, 1)

            act.wait_ge(px0_t, 2)
            copy(tok_l[0:L0, :, 1, :], bank[4][0:L0, :].rearrange("p (b n) -> p b n", b=B)).then_inc(px0_ev_act, 1)
            rows_turned(0)
            for n in range(1, CLS):
                rows_turned(n)
                values_made(n - 1)
            values_made(CLS - 1)

            def queries(n, src):
                act.wait_ge(q_mm, n + 1)
                if n:
                    act.wait_ge(q_ev, HG * n)
                    act.wait_ge(qc_ev, n)
                act.activation(q_sb[:, :], src[0:GH, 0:S], ACT.Copy, scale=SCALE).then_inc(q_in, 1)

            def exps(hh):
                h = hh % H
                act.wait_ge(max_ready, hh + 1)
                if hh >= H:
                    act.wait_ge(p_t, hh - H + 1)
                    act.wait_ge(rp_ready, hh // HG - 1)
                for i in range(HALVES):
                    act.activation(probs[:, h, i, :], bank[2 * (hh % 2) + i][:, 0:S], ACT.Exp,
                                   bias=nmax[:, h, i:i + 1], accum_out=den[:, h, i:i + 1]).then_inc(exp_ready, 1)

            def turned_probs(hh):
                h = hh % H
                act.wait_ge(p_t, hh + 1)
                if hh >= H:
                    act.wait_ge(pv_mm, hh // HG - G + 1)
                copy(pt[:, h, :, 0:N], bank[5][:, :].rearrange("p (j n) -> p j n", j=2)).then_inc(pt_act, 1)

            def class_exps(b, src):
                act.wait_ge(cmax_ready, b + 1)
                if b:
                    act.wait_ge(cp_t, b)
                act.activation(probs_c[:, :], src[0:H, 0:S], ACT.Exp, bias=nmax_c[:, :],
                               accum_out=den_c[:, :]).then_inc(cexp_ready, 1)

            def factors(n, src):
                act.wait_ge(rp_t, n + 1)
                if n:
                    act.wait_ge(ot_ready, n)
                copy(rpt[:, :, 0:N], src[:, :].rearrange("p (w n) -> p w n", w=2)).then_inc(rp_ev, 1)

            def turned_rows(b, src):
                _, n, m = tiles(b)
                act.wait_ge(xt2_t, b + 1)
                if b:
                    act.wait_ge(lg_mm, b)
                src = src[0:KH, :].rearrange("p (i t n) -> p i t n", i=2, t=2)
                copy(xt2[:, 0:n, :, 0:m], src[:, 0:n, :, 0:m]).then_inc(xt2_ev, 1)

            def route_exps(b, _):
                _, n, m = tiles(b)
                act.wait_ge(ntop_ready, b + 1)
                if b:
                    act.wait_ge(prob_ready, b)
                for i in range(n):
                    act.activation(prob_e[0:m, i, :], logits[0:m, i, :], ACT.Exp, bias=ntop[0:m, i:i + 1],
                                   accum_out=prob_s[0:m, i:i + 1]).then_inc(pexp_ready, 1)

            work = {"q": queries, "cs": class_exps, "f": factors, "xr": turned_rows, "rk": route_exps}

            def tasks(plan):
                for kind, n in plan:
                    if kind in work:
                        work[kind](n, SPARE[kind, n])

            act.wait_ge(k_in, 16)
            tasks(FIRST)
            for hh in range(len(PLAN)):
                if TURN_LAG <= hh < HEADS + TURN_LAG and hh % 2 == 1:
                    turned_probs(hh - TURN_LAG)
                if hh < HEADS:
                    exps(hh)
                tasks(PLAN[hh])

            def slot_turned(s):
                act.wait_ge(xt3_t, s + 1)
                copy(xt3[:, :, :], bank[2][0:KH, 0:2 * P].rearrange("p (t n) -> p t n", t=2)).then_inc(xt3_ev, 1)

            def slot_gate(s):
                act.wait_ge(up_mm, s + 1)
                act.activation(gate[:, :], bank[0][:, :], ACT.Silu).then_inc(gate_ready, 1)

            def slot_result(s):
                act.wait_ge(down_mm, s + 1)
                after_slots(act, y_ready, s)
                copy(o_bf[:, :], bank[4][:, 0:C]).then_inc(obf_ready, 1)

            def slot_turned_hidden(s):
                act.wait_ge(hid_t_t, s + 1)
                copy(hid_t[:, :, :], bank[3][:, :].rearrange("p (c n) -> p c n", c=HC)).then_inc(hid_t_ev, 1)

            used = used_slots(act)
            slot_turned(0)
            slot_gate(0)
            slot_turned(1)
            slot_turned_hidden(0)

            def slot_step(s, _=None):
                slot_gate(s)
                if not isinstance(s, int) or s + 1 < SLOTS:
                    slot_turned(s + 1)
                slot_result(s - 1)
                slot_turned_hidden(s)

            slot_step(1)
            slot_step(2)
            with act.Fori(0, (MIN_SLOTS - 3) // STEPS) as turn:
                for step in range(STEPS):
                    slot_step(turn * STEPS + 3 + step)
            while_used(act, used, MIN_SLOTS, slot_step, lambda s, _: slot_result(s))

        @block.vector
        def _(dve):
            done = [0]

            def then(ins):
                done[0] += 1
                ins.then_inc(dve_done, 1)
                dve.wait_ge(dve_done, done[0])

            dve.memset(tok_r[:, :], 0.0).then_inc(prep, 1)
            dve.memset(half_neg[:, :], -0.5).then_inc(prep, 1)
            then(dve.memset(empty[:, :, :], 0.0))
            dve.memset(empty[:, :, C + 3:C + 4].bitcast(I32), NO_ROW).then_inc(empty_ready, 1)
            then(dve.memset(wv_pad[:, :, :, :], 0.0))
            dve.memset(nmax[:, :, :], 0.0).then_inc(prep, 1)
            dve.memset(v_sb[:, :, :, :, :], 0.0).then_inc(prep, 1)

            def residual(tile, m, src):
                dve.tensor_tensor(h1[0:m, tile, :], src, bproj_sb[0:m, :], ALU.add).then_inc(h1_ready, 1)

            def plus_eps(t, n, m):
                dve.tensor_scalar(mv1[0:m, t:t + n, 1], mv1[0:m, t:t + n, 1], EPS, None, ALU.add).then_inc(var1_ready, 1)

            def by_image(dst, src, signal):
                dve.tensor_copy(dst.rearrange("p b (g v) -> p g b v", g=src.shape[1]),
                                src.rearrange("p g (b v) -> p g b v", b=B)).then_inc(signal, 1)

            def turned(dst, groups, rows_n, wait, signal):
                dve.wait_ge(wait, 1)
                dve.tensor_copy(dst.rearrange("p g b m -> p b g m"),
                                bank[5][0:rows_n, :].rearrange("p (b g m) -> p b g m", b=B, g=groups)).then_inc(signal, 1)

            def pick(j):
                pair = slice(2 * j, 2 * j + 2)
                dve.wait_ge(pick_mm, j + 1)
                if j:
                    dve.wait_ge(pick_done, j)
                at = 2 * (j % 2)
                dve.tensor_tensor(picked, psum[:, at:at + 2, 0:RUN * B * V0].rearrange("p i (t c) -> p i t c", t=RUN),
                                  place_hot[:, pair, :].unsqueeze(3).broadcast_to([P, 2, RUN, B * V0]),
                                  ALU.mult).then_inc(picked_ready, 1)
                dve.wait_ge(picked_ready, j + 1)
                dve.tensor_reduce(px0[:, 2 * GP - SELECTED + 2 * j:2 * GP - SELECTED + 2 * j + 2, :],
                                  picked.rearrange("p i t c -> p i c t"), AX_X, ALU.add).then_inc(pick_done, 1)

            def find_runs(j):
                pair = slice(2 * j, 2 * j + 2)
                dve.tensor_scalar(which[:, pair, :], which[:, pair, :], RUN.bit_length() - 1, None,
                                  ALU.logical_shift_right).then_inc(run_ready, 1)
                dve.wait_ge(run_ready, j + 1)
                dve.tensor_scalar(run_hot[:, pair, :], which[:, pair, :], counts_f[:, RUN:RUN + 1], None,
                                  ALU.is_equal).then_inc(run_hot_ready, 1)

            dve.wait_ge(counts_ready, 2)
            then(dve.tensor_copy(counts_f, counts.bitcast(I32)))
            dve.wait_ge(which_in, 16)
            for j in range(SELECTED // 2):
                find_runs(j)
            dve.wait_ge(small_in, 16 * 3)
            then(dve.bn_stats(stat1[0:B, CLS, :], cls_x[:, :]))
            then(dve.bn_aggr(mv1[0:B, CLS, :], stat1[0:B, CLS, :]))
            plus_eps(CLS, 1, B)
            dve.tensor_copy(lb_rep[:, :, :], lb_sb[:, :].unsqueeze(2).broadcast_to([EMB, 3, B * N2])).then_inc(lb_ready, 1)
            dve.wait_ge(idx_in, 16)
            at = GATHERS - SELECTED
            then(dve.tensor_scalar(in_run.bitcast(I32), idx_sb[:, at:GATHERS], RUN - 1, None, ALU.bitwise_and))
            then(dve.tensor_tensor(place_hot, in_run.bitcast(I32).unsqueeze(2).broadcast_to([P, SELECTED, RUN]),
                                   counts_f[:, 0:RUN].unsqueeze(1).broadcast_to([P, SELECTED, RUN]), ALU.is_equal))
            pick(0)
            pick(1)
            pick(2)
            dve.wait_ge(k_in, 16)
            dve.tensor_copy(tri_bf[:, :], k[:, K_TRI:K_TRI + P]).then_inc(consts_bf, 1)
            dve.tensor_copy(one_bf[:, :], k[:, K_ONE:K_ONE + P]).then_inc(consts_bf, 1)
            dve.wait_ge(px2_in, 16 * (GP // G2))
            by_image(px2b[:, :, :], px2[:, :, :], px2_by_image)
            pick(3)
            turned(px2t[:, :, :, :], G2, L2 // G2, px2_t, px2_ev)
            dve.wait_ge(px1_in, 16 * (GP // G1))
            by_image(px1b[:, :, :], px1[:, :, :], px1_by_image)
            pick(4)
            turned(px1t[:, :, :, :], G1, L1 // G1, px1_t, px1_ev)
            dve.wait_ge(wqkv_in, 16)
            dve.tensor_copy(wv_pad[:, :, :, 0:D],
                            wqkv_sb[:, :, 2 * C:3 * C].rearrange("p t (h d) -> p t h d", h=H)).then_inc(prep, 1)
            dve.wait_ge(rstd1_ready, 1)
            dve.tensor_scalar(xn1c[:, :], cls_x[:, :], mv1[0:B, CLS, 0:1], rstd1[0:B, CLS:TILES], ALU.subtract,
                              ALU.mult).then_inc(clsn, 1)
            dve.wait_ge(attn_w_in, 16 * 2)
            residual(CLS, B, cls_x[:, :])
            pick(5)
            dve.wait_ge(cls_t, 1)
            dve.tensor_copy(xt1[:, :, :, N], bank[5][0:KH, 0:2 * B].rearrange("p (t b) -> p t b", t=2)).then_inc(cls_ev, 1)
            pick(6)
            dve.wait_ge(vcls_mm, 1)
            dve.tensor_copy(vcls[:, :, :], bank[4][:, 0:G * B].rearrange("p (g b) -> p g b", g=G)).then_inc(vcls_ev, 1)

            for half in range(HALVES):
                dve.wait_ge(px0_in[half], 16 * (GP - half * SELECTED))
                if half:
                    dve.wait_ge(pick_done, SELECTED // 2)
                by_image(px0b[:, half, :, :], px0[:, half * GP:(half + 1) * GP, :], px0_by_image)
            dve.wait_ge(px0_t, 1)
            dve.tensor_copy(tok_l[0:L0, :, 0, :], bank[5][0:L0, :].rearrange("p (b n) -> p b n", b=B)).then_inc(px0_ev, 1)

            def token(n):
                b, half = divmod(n, HALVES)
                return bank[b][:, half * C:(half + 1) * C]

            for pair in range(2):
                tiles_of = range(pair * B, (pair + 1) * B)
                for n in tiles_of:
                    dve.wait_ge(tok_mm, n // HALVES + 1)
                    last = dve.bn_stats(stat1[:, n, :], token(n))
                then(last)
                for n in tiles_of:
                    last = dve.bn_aggr(mv1[:, n, :], stat1[:, n, :])
                then(last)
                plus_eps(pair * B, B, P)
            for pair in range(2):
                dve.wait_ge(rstd1_ready, 2 + pair)
                for n in range(pair * B, (pair + 1) * B):
                    if pair:
                        dve.wait_ge(xt1_t, n - B + 1)
                    dve.tensor_scalar(xn1[:, n % B, :], token(n), mv1[:, n, 0:1], rstd1[:, n:n + 1], ALU.subtract,
                                      ALU.mult).then_inc(xn1_ready, 1)
                for n in range(pair * B, (pair + 1) * B):
                    residual(n, P, token(n))

            def class_query(n, _):
                b, g = divmod(n, G)
                dve.wait_ge(q_in, n + 1)
                if b >= 2:
                    dve.wait_ge(csc_mm, b - 1)
                dve.tensor_scalar(q_cls[:, b % 2, g, :], k[0:GH, K_M8 + g * H:K_M8 + (g + 1) * H], q_sb[:, N:S],
                                  None, ALU.mult).then_inc(qc_ev, 1)

            def keys(n, src):
                b, g = divmod(n, G)
                dve.wait_ge(k_mm, n + 1)
                if b >= 2:
                    dve.wait_ge(sc_mm, H * (b - 1))
                    dve.wait_ge(csc_mm, b - 1)
                dve.tensor_copy(k_sb[:, b % 2, g, :], src[0:GH, 0:S]).then_inc(k_ev, 1)

            def class_max(b, src):
                dve.wait_ge(csc_mm, b + 1)
                if b:
                    dve.wait_ge(cexp_ready, b)
                dve.tensor_reduce(nmax_c[:, :], src[0:H, 0:S], AX_X, ALU.max, negate=True).then_inc(cmax_ready, 1)

            def class_factors(b):
                dve.wait_ge(cexp_ready, b + 1)
                if b:
                    dve.wait_ge(cp_t, b)
                then(dve.reciprocal(rp_c[:, 0:1], den_c[:, :]))
                dve.tensor_scalar(rp_c[:, 1:2], probs_c[:, N:S], rp_c[:, 0:1], None, ALU.mult).then_inc(crp_ready, 1)

            def class_turned(b, src):
                dve.wait_ge(cp_t, b + 1)
                dve.tensor_copy(rpc[:, b % 2, :, :],
                                src[:, 32:32 + 2 * G].rearrange("p (g w) -> p g w", g=G)).then_inc(rpc_ready, 1)
                if b:
                    dve.wait_ge(col_ready, b)
                dve.tensor_copy(col[:, :, :], src[:, 0:HALVES * H].rearrange("p (j h) -> p j h", j=HALVES))\
                   .then_inc(cp_ev, 1)

            def class_columns(b):
                dve.wait_ge(cp_ev, b + 1)
                if b:
                    dve.wait_ge(pv_mm, G * b)
                dve.tensor_copy(pt[:, :, :, N].rearrange("p h j -> p j h"), col[:, :, :]).then_inc(col_ready, 1)

            def maxes(hh):
                h = hh % H
                dve.wait_ge(sc_mm, hh + 1)
                if hh >= H:
                    dve.wait_ge(exp_ready, 2 * (hh - H + 1))
                at = 2 * (hh % 2)
                dve.tensor_reduce(nmax[:, h, :], psum[:, at:at + HALVES, 0:S], AX_X, ALU.max, negate=True)\
                   .then_inc(max_ready, 1)

            def turned_probs(hh):
                h = hh % H
                dve.wait_ge(p_t, hh + 1)
                if hh >= H:
                    dve.wait_ge(pv_mm, hh // HG - G + 1)
                dve.tensor_copy(pt[:, h, :, 0:N], bank[5][:, :].rearrange("p (j n) -> p j n", j=2)).then_inc(pt_dve, 1)

            def ratios(n):
                g = n % G
                heads = slice(g * HG, (g + 1) * HG)
                dve.wait_ge(exp_ready, 2 * HG * (n + 1))
                if n:
                    dve.wait_ge(rp_t, n)
                then(dve.reciprocal(rp[:, 0, :, heads], den[:, heads, :].rearrange("p h i -> p i h")))
                dve.tensor_tensor(rp[:, 1, :, heads], rp[:, 0, :, heads],
                                  probs[:, heads, :, N].rearrange("p h i -> p i h"), ALU.mult).then_inc(rp_ready, 1)
                dve.wait_ge(rp_ready, n + 1)
                dve.tensor_copy(rp_rows[:, :, :, :].rearrange("p w i (h d) -> p (w i) h d", h=HG),
                                rp[:, :, :, heads].rearrange("p w i h -> p (w i) h").unsqueeze(3)
                                .broadcast_to([P, 2 * HALVES, HG, HP])).then_inc(rp_rows_ready, 1)

            def finish_group(n):
                b, g = divmod(n, G)
                dve.wait_ge(rp_ev, n + 1)
                dve.wait_ge(rpc_ready, b + 1)
                then(dve.tensor_copy(rpt[:, :, N], rpc[:, b % 2, g, :]))
                dve.wait_ge(pv_mm, n + 1)
                if n:
                    dve.wait_ge(ot_ready, n)
                dve.tensor_tensor(part[:, :], bank[4][:, 0:S], rpt[:, 0, :], ALU.mult).then_inc(part_ready, 1)
                dve.wait_ge(part_ready, n + 1)
                dve.scalar_tensor_tensor(out=ot[:, b, g, :], in0=rpt[:, 1, :], scalar=vcls[:, g, b:b + 1],
                                         in1=part[:, :], op0=ALU.mult, op1=ALU.add).then_inc(ot_ready, 1)

            def second_residual(b, src):
                t, n, m = tiles(b)
                dve.wait_ge(proj_mm, b + 1)
                dve.tensor_tensor(rows[0:m, t:t + n, 0:C], src[0:m, 0:n * C].rearrange("p (i c) -> p i c", i=n),
                                  h1[0:m, t:t + n, :], ALU.add).then_inc(h2_ready, 1)
                dve.wait_ge(h2_ready, b + 1)
                for i in range(n):
                    last = dve.bn_stats(stat2[0:m, i, :], rows[0:m, t + i, 0:C])
                then(last)
                for i in range(n):
                    last = dve.bn_aggr(rows[0:m, t + i, C:C + 2], stat2[0:m, i, :])
                then(last)
                dve.tensor_scalar(vare[0:m, t:t + n], rows[0:m, t:t + n, C + 1], EPS, None, ALU.add)\
                   .then_inc(var2_ready, 1)

            def second_norm(b):
                t, n, m = tiles(b)
                dve.wait_ge(rstd2_ready, b + 1)
                if b:
                    dve.wait_ge(xt2_t, b)
                for i in range(n):
                    last = dve.tensor_scalar(xn2[0:m, i, :], rows[0:m, t + i, 0:C], rows[0:m, t + i, C:C + 1],
                                             rows[0:m, t + i, C + 1:C + 2], ALU.subtract, ALU.mult)
                last.then_inc(xn2_ready, 1)

            def choose(b, src):
                t, n, m = tiles(b)
                dve.wait_ge(lg_mm, b + 1)
                if b:
                    dve.wait_ge(pexp_ready, HALVES * b)
                dve.tensor_tensor(logits[0:m, 0:n, :], src[0:m, 0:n * E].rearrange("p (i e) -> p i e", i=n),
                                  rb_sb[0:m, :].unsqueeze(1).broadcast_to([m, n, E]), ALU.add).then_inc(lg_ready, 1)
                dve.wait_ge(lg_ready, b + 1)
                for i in range(n):
                    last = dve.max(top[0:m, i, :], logits[0:m, i, :])
                then(last)
                dve.tensor_scalar(ntop[0:m, 0:n], top[0:m, 0:n, 0], -1.0, None, ALU.mult).then_inc(ntop_ready, 1)
                for i in range(n):
                    last = dve.max_index(topi[0:m, i, :], top[0:m, i, :], logits[0:m, i, :])
                then(last)
                for i in range(n):
                    last = dve.tensor_scalar(chosen[0:m, t + i, :], k[0:m, K_E:K_E + E], topi[0:m, i, 0:1], None,
                                             ALU.is_equal)
                last.then_inc(chosen_ready, 1)

            def place_rows(b, src):
                t, n, m = tiles(b)
                dve.wait_ge(rank_mm, b + 1)
                dve.tensor_tensor(place[0:m, 0:n, :], src[0:m, 0:n * E].rearrange("p (i e) -> p i e", i=n),
                                  k[0:m, K_BASE:K_BASE + E].unsqueeze(1).broadcast_to([m, n, E]),
                                  ALU.add).then_inc(place_ready, 1)
                dve.wait_ge(place_ready, b + 1)
                then(dve.tensor_tensor(place2[0:m, 0:n, :], place[0:m, 0:n, :], chosen[0:m, t:t + n, :], ALU.mult))
                then(dve.tensor_reduce(pos[0:m, t:t + n], place2[0:m, 0:n, :], AX_X, ALU.add))
                dve.wait_ge(pexp_ready, min(HALVES * (b + 1), TILES))
                dve.reciprocal(rows[0:m, t:t + n, C + 2], prob_s[0:m, 0:n]).then_inc(prob_ready, 1)
                dve.tensor_copy(pos_i[0:m, t:t + n], pos[0:m, t:t + n]).then_inc(pos_ready, 1)

            def fill_slots(_, src):
                dve.wait_ge(cnt_mm, 1)
                one = k[0:1, :]

                def grid(at, a, c):
                    return one[:, at:at + a * c].rearrange("p (a c) -> p a c", a=a)

                over = nt[:, 0:E * NJ].rearrange("p (a c) -> p a c", a=E)
                n_slots, step, end = (nt[:, E * NJ + i * E:E * NJ + (i + 1) * E] for i in range(3))
                then(dve.tensor_tensor(over, src[0:1, 0:E].unsqueeze(2).broadcast_to([1, E, NJ]), grid(K_J, E, NJ),
                                       ALU.is_gt))
                then(dve.tensor_reduce(n_slots, over, AX_X, ALU.add))
                sums = upto[:, 0:E * E].rearrange("p (a c) -> p a c", a=E)
                then(dve.tensor_tensor(sums, n_slots.unsqueeze(1).broadcast_to([1, E, E]), grid(K_LE, E, E), ALU.mult))
                then(dve.tensor_reduce(end, sums, AX_X, ALU.add))
                le_g = le[:, :].rearrange("p (a c) -> p a c", a=SLOTS)
                then(dve.tensor_tensor(le_g, end.unsqueeze(1).broadcast_to([1, SLOTS, E]), grid(K_S, SLOTS, E),
                                       ALU.is_le))
                then(dve.tensor_reduce(slot_f[:, 0, :], le_g, AX_X, ALU.add))
                then(dve.tensor_scalar(step, n_slots, -float(P), float(REG), ALU.mult, ALU.add))
                wle_g = wle[:, :].rearrange("p (a c) -> p a c", a=SLOTS)
                then(dve.tensor_tensor(wle_g, le_g, step.unsqueeze(1).broadcast_to([1, SLOTS, E]), ALU.mult))
                then(dve.tensor_reduce(slot_f[:, 1, :], wle_g, AX_X, ALU.add))
                then(dve.tensor_tensor(slot_g[:, :], slot_f[:, 1, :], one[:, K_S128:K_S128 + SLOTS], ALU.add))
                dve.tensor_copy(slot_i[:, 2, 0:1], end[:, E - 1:E])
                dve.tensor_scalar(slot_i[:, 0, :], slot_f[:, 0, :], float(E - 1), None, ALU.min)
                dve.tensor_scalar(slot_i[:, 1, :], slot_g[:, :], float(PAD_ROW), None, ALU.min).then_inc(slots_ready, 1)

            work = {"q": class_query, "k": keys, "cs": class_max, "ct": class_turned,
                    "pj": second_residual, "lg": choose, "rk": place_rows, "cn": fill_slots}

            dve.wait_ge(rout_w_in, 16 * 2)
            for kind, n in FIRST:
                work[kind](n, SPARE[kind, n])
            for hh in range(len(PLAN)):
                if hh < HEADS:
                    maxes(hh)
                for kind, n in PLAN[hh + 1] if hh < HEADS else []:
                    if kind == "ct":
                        class_factors(n)
                if TURN_LAG <= hh < HEADS + TURN_LAG and hh % 2 == 0:
                    turned_probs(hh - TURN_LAG)
                if HG <= hh <= HEADS and hh % HG == 0:
                    ratios(hh // HG - 1)
                if hh < HEADS and hh % H == (VALUES_LAG if hh < H else 3):
                    class_columns(hh // H)
                if hh >= VALUES_LAG and (hh - VALUES_LAG) % HG == 0:
                    finish_group((hh - VALUES_LAG) // HG)
                if H < hh < HEADS and hh % H == 5:
                    second_norm(hh // H - 1)
                for kind, n in PLAN[hh]:
                    if kind == "xr" and hh > HEADS:
                        second_norm(n)
                    if kind in work:
                        work[kind](n, SPARE[kind, n])

            def slot_norm(s):
                dve.wait_ge(xs_in, (s + 1) * 16)
                after_slots(dve, xt3_t, s)
                dve.tensor_scalar(xn3[:, :], xs[:, bass.ds(s * ROW, C)], xs[:, bass.ds(s * ROW + C, 1)],
                                  xs[:, bass.ds(s * ROW + C + 1, 1)], ALU.subtract, ALU.mult).then_inc(xn3_ready, 1)

            def slot_hidden(s):
                dve.wait_ge(gate_ready, s + 1)
                after_slots(dve, hid_t_t, s)
                dve.tensor_tensor(hid[:, :], gate[:, :], bank[1][:, :], ALU.mult).then_inc(hid_ready, 1)

            def slot_rows(s):
                dve.wait_ge(obf_ready, s + 1)
                after_slots(dve, y_out, s, 16)
                dve.tensor_copy(y_row[:, :], xs_i[:, bass.ds(s * ROW + C + 3, 1)])
                dve.scalar_tensor_tensor(out=y[:, :], in0=o_bf[:, :], scalar=xs[:, bass.ds(s * ROW + C + 2, 1)],
                                         in1=xs[:, bass.ds(s * ROW, C)], op0=ALU.mult, op1=ALU.add)\
                   .then_inc(y_ready, 1)

            used = used_slots(dve)
            slot_norm(0)
            slot_norm(1)
            slot_hidden(0)

            def slot_step(s, _=None):
                if not isinstance(s, int) or s + 1 < SLOTS:
                    slot_norm(s + 1)
                slot_hidden(s)
                slot_rows(s - 1)

            slot_step(1)
            slot_step(2)
            with dve.Fori(0, (MIN_SLOTS - 3) // STEPS) as turn:
                for step in range(STEPS):
                    slot_step(turn * STEPS + 3 + step)
            while_used(dve, used, MIN_SLOTS, slot_step, lambda s, _: slot_rows(s))


def shape_constants():
    import numpy as np

    k = np.zeros((P, K_END), np.float32)
    p = np.arange(P)
    k[:, K_ID:K_ID + P] = np.eye(P)

    def interpolation(m):
        at = np.clip((np.arange(N) + 0.5) * (m / N) - 0.5, 0.0, m - 1)
        lo = np.floor(at).astype(int)
        w = np.zeros((m, N), np.float32)
        np.add.at(w, (lo, np.arange(N)), 1.0 - (at - lo))
        np.add.at(w, (np.minimum(lo + 1, m - 1), np.arange(N)), at - lo)
        return w

    w1, w2 = interpolation(N1), interpolation(N2)
    for odd in range(2):
        k[odd * N1:(odd + 1) * N1, K_I1 + odd * N:K_I1 + (odd + 1) * N] = w1
    for h in range(HG):
        k[h * D:(h + 1) * D, K_MQ + h] = 1.0
        for g in range(G):
            k[h * D:(h + 1) * D, K_M8 + g * H + g * HG + h] = 1.0
    for g in range(G):
        for h in range(HG):
            k[g * HG + h, K_SEL + g * P + h * HP:K_SEL + g * P + (h + 1) * HP] = 1.0
    k[:, K_E:K_E + E] = np.arange(E)
    k[:, K_BASE:K_BASE + E] = np.arange(E) * REG
    k[:, K_TRI:K_TRI + P] = p[:, None] < p[None, :]
    k[:, K_ONE:K_ONE + P] = 1.0
    k[0, K_J:K_J + E * NJ] = np.tile(np.arange(NJ) * P, E)
    k[0, K_LE:K_LE + E * E] = (np.arange(E)[None, :] <= np.arange(E)[:, None]).ravel()
    k[0, K_S:K_S + SLOTS * E] = np.repeat(np.arange(SLOTS), E)
    k[0, K_S128:K_S128 + SLOTS] = np.arange(SLOTS) * P
    two = np.zeros((P - L0, B, N), np.float32)
    for b in range(B):
        two[EMB - L0 + b * N2:EMB - L0 + (b + 1) * N2, b] = w2
    return k, two.reshape(P - L0, B * N)


def kernel(x, cls_tok, L0_tok_W0, L0_tok_b0, L0_tok_W1, L0_tok_b1, L0_tok_W2, L0_tok_b2, L0_tok_Wf, L0_tok_bf,
           L0_tok_idx0, L0_tok_idx1, L0_tok_idx2, L0_attn_w_qkv, L0_attn_w_proj, L0_attn_b_proj, L0_ffn_router_w,
           L0_ffn_router_b, L0_ffn_w1, L0_ffn_w2, L0_ffn_w3):
    import concourse.bacc as bacc
    import numpy as np
    from concourse.bass_utils import run_bass_kernel_spmd

    x = np.asarray(x)

    def patches(p):
        n = GRID // p
        t = x.reshape(B, CH, n, p, n, p).transpose(2, 4, 0, 3, 5, 1)
        return t.reshape(n * n, B * p * p * CH)

    idx0, idx1, idx2 = (np.asarray(a) for a in (L0_tok_idx0, L0_tok_idx1, L0_tok_idx2))
    idx = np.concatenate([
        idx2.reshape(N2, G2, GP // G2).transpose(1, 0, 2).reshape(P, GP // G2),
        idx1.reshape(N1, G1, GP // G1).transpose(1, 0, 2).reshape(P, GP // G1),
        idx0.reshape(HALVES, P, GP).transpose(1, 0, 2).reshape(P, HALVES * GP),
    ], axis=1)
    last = idx0.reshape(HALVES, P, GP)[HALVES - 1, :, GP - SELECTED:].T
    wproj = np.zeros((HG, HP, G, C), np.float32)
    wproj[:, 0:D] = np.asarray(L0_attn_w_proj).reshape(G, HG, D, C).transpose(1, 2, 0, 3)
    consts, interp2 = shape_constants()
    arrays = {
        "pix0": patches(1), "pix1": patches(2), "pix2": patches(4), "idx": idx, "idx_row": last.reshape(1, SELECTED * P),
        "lw": np.concatenate([np.asarray(a) for a in (L0_tok_W0, L0_tok_W1, L0_tok_W2)], axis=1),
        "wft": np.asarray(L0_tok_Wf).reshape(C, 3, EMB).transpose(2, 1, 0),
        "lb": np.stack([np.asarray(a) for a in (L0_tok_b0, L0_tok_b1, L0_tok_b2)], axis=1),
        "bf": np.asarray(L0_tok_bf).reshape(1, C), "cls_tok": np.asarray(cls_tok).reshape(1, C),
        "wqkv": L0_attn_w_qkv, "wproj": wproj.reshape(P, G, C),
        "bproj": np.asarray(L0_attn_b_proj).reshape(1, C), "rw": L0_ffn_router_w,
        "rb": np.asarray(L0_ffn_router_b).reshape(1, E), "w1": L0_ffn_w1, "w2": L0_ffn_w2, "w3": L0_ffn_w3,
        "consts": consts, "interp2": interp2,
    }
    arrays = {name: np.ascontiguousarray(a) for name, a in arrays.items()}
    nc = bacc.Bacc("TRN2", target_bir_lowering=False, num_devices=1)
    args = [nc.dram_tensor(name, a.shape, mybir.dt.from_np(a.dtype), kind="ExternalInput").ap()
            for name, a in arrays.items()]
    out = nc.dram_tensor("out", (B * S, C), F32, kind="ExternalOutput").ap()
    build(nc, *args, out)
    got = run_bass_kernel_spmd(nc, [arrays], core_ids=[0]).results[0]["out"]
    return got.reshape(B, S, C)
```
